# Optimizing a Trainium2 kernel written in Bass

```python
import numpy as np
import jax
import jax.numpy as jnp

def _softmax(x, axis=-1):
    return jax.nn.softmax(x, axis=axis)

def _gelu(x):
    return jax.nn.gelu(x, approximate=True)

def _silu(x):
    return jax.nn.silu(x)

def _sigmoid(x):
    return jax.nn.sigmoid(x)

def _layernorm(x, axis=-1, eps=1e-05):
    m = jnp.mean(x, axis=axis, keepdims=True)
    v = jnp.var(x, axis=axis, keepdims=True)
    return (x - m) / jnp.sqrt(v + eps)

def _scatter_add(tgt, idx, src, axis=0):
    return tgt.at[idx].add(src)

def _segment_sum(src, seg, n):
    return jax.ops.segment_sum(src, seg, n)
kernel_name = 'mk_macaron_d1_jaxref_r8_a1b366'

def setup_inputs(seed: int=0):
    np.random.seed(seed)
    _w = jnp.asarray

    def _L0_attn_setup():
        import jax, jax.numpy as jnp
        import numpy as np
        import math
        B, L, D, H = (32, 64, 512, 32)
        HD = D // H
        key = jax.random.key(seed)
        ks = jax.random.split(key, 9)
        s = 1.0 / math.sqrt(D)
        return {'x': jax.random.normal(ks[0], (B, L, D), jnp.float32), 'Wq': jax.random.normal(ks[1], (D, D), jnp.float32) * s, 'bq': jax.random.normal(ks[2], (D,), jnp.float32) * s, 'Wk': jax.random.normal(ks[3], (D, D), jnp.float32) * s, 'bk': jax.random.normal(ks[4], (D,), jnp.float32) * s, 'Wv': jax.random.normal(ks[5], (D, D), jnp.float32) * s, 'bv': jax.random.normal(ks[6], (D,), jnp.float32) * s, 'Wo': jax.random.normal(ks[7], (D, D), jnp.float32) * s, 'bo': jax.random.normal(ks[8], (D,), jnp.float32) * s}
    _L0_attn_in = _L0_attn_setup()

    def _L0_ffn_setup():
        import jax, jax.numpy as jnp
        import numpy as np
        B, T, D_IN, D_OUT = (8, 256, 512, 512)
        N_LORAS, RANK = (16, 32)
        SCALING = 1.0
        key = jax.random.key(seed)
        ks = jax.random.split(key, 8)
        std = 1.0 / D_IN ** 0.5
        x = jax.random.normal(ks[0], (B, T, D_IN), dtype=jnp.float32)
        idx = jax.random.randint(ks[1], (B,), 0, N_LORAS)
        gate = jax.nn.one_hot(idx, N_LORAS, dtype=jnp.float32)
        kernel = jax.random.normal(ks[2], (D_IN, D_OUT), dtype=jnp.float32) * std
        bias = jnp.zeros((D_OUT,), dtype=jnp.float32)
        lora_A = jax.random.normal(ks[3], (N_LORAS, RANK, D_IN), dtype=jnp.float32) * std
        lora_B = jax.random.normal(ks[4], (N_LORAS, D_OUT, RANK), dtype=jnp.float32) * 0.01
        lora_A_shared = jax.random.normal(ks[5], (RANK, D_IN), dtype=jnp.float32) * std
        lora_B_shared = jax.random.normal(ks[6], (D_OUT, RANK), dtype=jnp.float32) * 0.01
        return {'x': x, 'gate': gate, 'kernel': kernel, 'bias': bias, 'lora_A': lora_A, 'lora_B': lora_B, 'lora_A_shared': lora_A_shared, 'lora_B_shared': lora_B_shared}
    _L0_ffn_in = _L0_ffn_setup()
    _d = {'L0_attn_x': _L0_attn_in['x'], 'L0_attn_Wq': _L0_attn_in['Wq'], 'L0_attn_bq': _L0_attn_in['bq'], 'L0_attn_Wk': _L0_attn_in['Wk'], 'L0_attn_bk': _L0_attn_in['bk'], 'L0_attn_Wv': _L0_attn_in['Wv'], 'L0_attn_bv': _L0_attn_in['bv'], 'L0_attn_Wo': _L0_attn_in['Wo'], 'L0_attn_bo': _L0_attn_in['bo'], 'L0_ffn_gate': _L0_ffn_in['gate'], 'L0_ffn_kernel': _L0_ffn_in['kernel'], 'L0_ffn_bias': _L0_ffn_in['bias'], 'L0_ffn_lora_A': _L0_ffn_in['lora_A'], 'L0_ffn_lora_B': _L0_ffn_in['lora_B'], 'L0_ffn_lora_A_shared': _L0_ffn_in['lora_A_shared'], 'L0_ffn_lora_B_shared': _L0_ffn_in['lora_B_shared']}
    _x0 = _d['L0_attn_x']
    _d['L0_attn_x'] = jax.random.normal(jax.random.fold_in(jax.random.key(seed), 1), (2, 1024, 512), dtype=_x0.dtype)
    del _x0
    return _d

def reference(L0_attn_x, L0_attn_Wq, L0_attn_bq, L0_attn_Wk, L0_attn_bk, L0_attn_Wv, L0_attn_bv, L0_attn_Wo, L0_attn_bo, L0_ffn_gate, L0_ffn_kernel, L0_ffn_bias, L0_ffn_lora_A, L0_ffn_lora_B, L0_ffn_lora_A_shared, L0_ffn_lora_B_shared):

    def _L0_attn_ref(x, Wq, bq, Wk, bk, Wv, bv, Wo, bo):
        import jax, jax.numpy as jnp
        import numpy as np
        import math
        B, L, D, H = (32, 64, 512, 32)
        HD = D // H
        b, l, d = x.shape
        h, hd = (H, HD)
        q = (x @ Wq.T + bq).reshape(b, l, h, hd).transpose(0, 2, 1, 3)
        k = (x @ Wk.T + bk).reshape(b, l, h, hd).transpose(0, 2, 1, 3)
        v = (x @ Wv.T + bv).reshape(b, l, h, hd).transpose(0, 2, 1, 3)
        scores = jnp.einsum('bhqd,bhkd->bhqk', q, k) / math.sqrt(hd)
        causal = jnp.tril(jnp.ones((l, l), bool))
        scores = jnp.where(causal, scores, -jnp.inf)
        att = jax.nn.softmax(scores, axis=-1)
        out = jnp.einsum('bhqk,bhkd->bhqd', att, v)
        out = out.transpose(0, 2, 1, 3).reshape(b, l, d)
        return out @ Wo.T + bo

    def _L0_ffn_ref(x, gate, kernel, bias, lora_A, lora_B, lora_A_shared, lora_B_shared):
        import jax, jax.numpy as jnp
        import numpy as np
        B, T, D_IN, D_OUT = (8, 256, 512, 512)
        N_LORAS, RANK = (16, 32)
        SCALING = 1.0
        base_out = jnp.matmul(x, kernel) + bias
        b = gate.shape[0]
        x_flat = x.reshape(b, -1, x.shape[-1])
        A_eff = jnp.einsum('bn,nri->bri', gate, lora_A)
        B_eff = jnp.einsum('bn,nor->bor', gate, lora_B)
        Ax = jnp.einsum('bri,bti->btr', A_eff, x_flat)
        delta_flat = jnp.einsum('bor,btr->bto', B_eff, Ax)
        Ax_s = jnp.einsum('ri,bti->btr', lora_A_shared, x_flat)
        delta_flat = delta_flat + jnp.einsum('or,btr->bto', lora_B_shared, Ax_s)
        delta = delta_flat.reshape(x.shape[:-1] + (kernel.shape[-1],))
        return base_out + (SCALING * delta).astype(base_out.dtype)
    x = L0_attn_x
    x = x + 0.5 * _L0_ffn_ref(_layernorm(x, axis=-1), L0_ffn_gate, L0_ffn_kernel, L0_ffn_bias, L0_ffn_lora_A, L0_ffn_lora_B, L0_ffn_lora_A_shared, L0_ffn_lora_B_shared)
    x = x + _L0_attn_ref(_layernorm(x, axis=-1), L0_attn_Wq, L0_attn_bq, L0_attn_Wk, L0_attn_bk, L0_attn_Wv, L0_attn_bv, L0_attn_Wo, L0_attn_bo)
    x = x + 0.5 * _L0_ffn_ref(_layernorm(x, axis=-1), L0_ffn_gate, L0_ffn_kernel, L0_ffn_bias, L0_ffn_lora_A, L0_ffn_lora_B, L0_ffn_lora_A_shared, L0_ffn_lora_B_shared)
    return x

_drawn_inputs = setup_inputs


def setup_inputs(seed=0):
    import zlib

    import numpy as np

    out = dict(_drawn_inputs(seed))
    spreads = {'L0_ffn_bias': (0.0, 0.1)}
    factors = {'L0_attn_bq': 8.0, 'L0_attn_bk': 8.0}
    for name, (base, spread) in spreads.items():
        noise = np.random.default_rng([zlib.crc32(name.encode()), seed]).standard_normal(out[name].shape)
        drawn = base * np.exp(spread * noise) if base else spread * noise
        out[name] = jnp.asarray(drawn.astype(out[name].dtype))
    for name, factor in factors.items():
        out[name] = (out[name] * factor).astype(out[name].dtype)
    return out
```

```python
from contextlib import ExitStack

import concourse.bass as bass
from concourse import mybir

F32 = mybir.dt.float32
F32R = mybir.dt.float32r
BF16 = mybir.dt.bfloat16
ALU = mybir.AluOpType
ACT = mybir.ActivationFunctionType
AX = mybir.AxisListType

P = 128
D = 512
NI = D // P
HD = 16
HEADS = D // HD
TOK = 2048
SEQ = 1024
BATCH = TOK // SEQ
CH = 512
CT = CH // P
NCH = TOK // CH
GROUPS = 8
GT = TOK // GROUPS // P
GC = GROUPS // NCH
LORAS = 16
RANK = 32
LCH = LORAS * RANK // P
EPS = 1e-5
FMIN = -3.0e38

HG = 4
NG = HEADS // HG
UNITS = BATCH * NG
VC = HD + 1
PARTS = 3
TERMS = [(0, 0), (0, 1), (0, 2), (1, 0), (1, 1), (2, 0)]
KROWS = HD * len(TERMS)
SROWS = KROWS + 2
NPACK = 3
LOADS = 3 * len(TERMS) + 1
QT = SEQ // P
STEPS = [(c, kt) for c in range(2) for kt in range(CT * (c + 1))]
NS = len(STEPS)
DIAG = [s for s, (c, kt) in enumerate(STEPS) if kt >= CT * c]
PBUF = 3


class Events:

    def __init__(self, sem, step=1, ahead=0):
        self.sem, self.step, self.ahead = sem, step, ahead

    def __getitem__(self, n):
        return self.sem, (n + (self.ahead + 1)) * self.step


def give_ahead(eng, events):
    for e in events:
        if e.ahead:
            eng.sem_inc(e.sem, e.ahead * e.step)


def project(pe, psum, left, right, done):
    terms = [(0, 1), (1, 0), (0, 0)]
    for n, (a, b) in enumerate(terms):
        for ic in range(NI):
            last = pe.matmul(psum, left(a, ic), right(b, ic), start=(n == 0 and ic == 0),
                             stop=(n == len(terms) - 1 and ic == NI - 1))
    last.then_inc(done, 1)


def build(nc, x, wqT, wkT, wvT, woT, bq, bk, bv, bo, gate, ffn_w, ffn_b, lora_a, lora_b, lora_as, lora_bs, out):
    with ExitStack() as whole:
        def dram(name, shape, dt):
            return nc.dram_tensor(name, shape, dt, kind="Internal").ap()

        lora_scr = dram("lora_scr", (GROUPS, RANK, 2 * D), F32)
        x1_scr = dram("x1_scr", (TOK, D), F32)
        q_scr = dram("q_scr", (PARTS, BATCH * D, SEQ), BF16)
        k_scr = dram("k_scr", (PARTS, BATCH * D, SEQ), BF16)
        v_scr = dram("v_scr", (UNITS, SEQ, HG * VC), F32)
        o_scr = dram("o_scr", (UNITS, SEQ, HG * HD), F32)

        ident = whole.enter_context(nc.sbuf_tensor("ident", [P, P], F32))
        causal = whole.enter_context(nc.sbuf_tensor("causal", [P, CH], F32))
        ps = whole.enter_context(nc.psum_tensor("ps", [P, 8, 512], F32))
        small = whole.enter_context(nc.sbuf_tensor("small", [P, 8], F32))
        neg_half, eps = small[:, 0:1], small[:, 1:2]

        stage_0(nc, ps, ident, causal, neg_half, eps, gate, lora_a, lora_b, lora_scr)
        stage_a(nc, ps, ident, neg_half, eps, x, wqT, wkT, wvT, bq, bk, bv, bo, ffn_w, ffn_b, lora_as, lora_bs,
                lora_scr, x1_scr, q_scr, k_scr, v_scr)
        stage_b(nc, ps, ident, causal, q_scr, k_scr, v_scr, o_scr)
        stage_c(nc, ps, ident, neg_half, eps, woT, ffn_w, ffn_b, lora_as, lora_bs, lora_scr, x1_scr, o_scr, out)


def stage_0(nc, ps, ident, causal, neg_half, eps, gate, lora_a, lora_b, lora_scr):
    with ExitStack() as ctx:
        def sb(name, shape, dt=F32):
            return ctx.enter_context(nc.sbuf_tensor(name, shape, dt))

        def sem(name):
            return ctx.enter_context(nc.semaphore(name))

        ab = sb("ab", [P, 2, LCH, D])
        gate_rows = sb("gate_rows", [P, LCH, GROUPS])
        delta = sb("delta", [P, RANK])
        spread = sb("spread", [P, LCH, GROUPS, RANK])
        eff = sb("eff", [P, 2, 2, D])

        gate_in, a_in, b_in = sem("gate_in"), sem("a_in"), sem("b_in")
        zeroed, consts, spread_ok = sem("zeroed"), sem("consts"), sem("spread_ok")
        eff_made, eff_taken, eff_out = sem("eff_made"), sem("eff_taken"), sem("eff_out")
        HALF = GROUPS // 2

        block = ctx.enter_context(nc.Block())

        @block.sync
        def _(sp):
            sp.dma_start(gate_rows[:, :, :], gate.rearrange("(c p) b -> p c b", p=P)).then_inc(gate_in, 16)
            sp.dma_start(ab[:, 0, :, :], lora_a.rearrange("(c p) d -> p c d", p=P)).then_inc(a_in, 16)
            sp.dma_start(ab[:, 1, :, :], lora_b.rearrange("(c p) d -> p c d", p=P)).then_inc(b_in, 16)
            for half in range(2):
                for f in range(2):
                    sp.wait_ge(eff_taken, 2 * half + f + 1)
                    dst = lora_scr[half * HALF:(half + 1) * HALF, :, f * D:(f + 1) * D]
                    sp.dma_start(dst.rearrange("b r d -> (b r) d"), eff[:, half, f, :]).then_inc(eff_out, 16)
            sp.wait_ge(eff_out, 16 * 4)

        @block.gpsimd
        def _(pool):
            pool.memset(ident[:, :], 0.0).then_inc(zeroed, 1)
            pool.memset(delta[:, :], 0.0).then_inc(zeroed, 1)
            pool.memset(causal[:, :], 0.0).then_inc(zeroed, 1)
            pool.memset(neg_half, -0.5).then_inc(consts, 1)
            pool.memset(eps, EPS).then_inc(consts, 1)
            pool.wait_ge(zeroed, 3)
            pool.affine_select(out=ident[:, :], in_=ident[:, :], compare_op=ALU.not_equal, fill=1.0, base=0,
                               pattern=[[-1, P]], channel_multiplier=1).then_inc(consts, 1)
            pool.affine_select(out=causal[:, CH - P:CH], in_=causal[:, CH - P:CH], compare_op=ALU.is_ge,
                               fill=FMIN, base=0, pattern=[[-1, P]], channel_multiplier=1).then_inc(consts, 1)
            for n in range(P // RANK):
                pool.wait_ge(zeroed, 3 + n)
                pool.affine_select(out=delta[:, :], in_=delta[:, :], compare_op=ALU.not_equal, fill=1.0,
                                   base=-n * RANK, pattern=[[-1, RANK]], channel_multiplier=1).then_inc(zeroed, 1)

        @block.vector
        def _(dve):
            dve.wait_ge(zeroed, 3 + P // RANK)
            dve.wait_ge(gate_in, 16)
            for c in range(LCH):
                dve.tensor_tensor(spread[:, c, :, :],
                                  delta[:, :].unsqueeze(1).to_broadcast([P, GROUPS, RANK]),
                                  gate_rows[:, c, :].unsqueeze(2).to_broadcast([P, GROUPS, RANK]),
                                  ALU.mult).then_inc(spread_ok, 1)
            for half in range(2):
                for f in range(2):
                    n = 2 * half + f
                    dve.wait_ge(eff_made, n + 1)
                    dve.tensor_copy(eff[:, half, f, :], ps[:, n, :]).then_inc(eff_taken, 1)

        @block.tensor
        def _(pe):
            pe.wait_ge(spread_ok, LCH)
            for half in range(2):
                for f, arrived in enumerate((a_in, b_in)):
                    pe.wait_ge(arrived, 16)
                    for c in range(LCH):
                        g = spread[:, c, half * HALF:(half + 1) * HALF, :].rearrange("p b r -> p (b r)")
                        last = pe.matmul(ps[:, 2 * half + f, :], g, ab[:, f, c, :], start=(c == 0),
                                         stop=(c == LCH - 1))
                    last.then_inc(eff_made, 1)


def stage_a(nc, ps, ident, neg_half, eps, x, wqT, wkT, wvT, bq, bk, bv, bo, ffn_w, ffn_b, lora_as, lora_bs,
            lora_scr, x1_scr, q_scr, k_scr, v_scr):
    with ExitStack() as ctx:
        every = []

        def sb(name, shape, dt=F32):
            return ctx.enter_context(nc.sbuf_tensor("a_" + name, shape, dt))

        def events(name, step=1, ahead=0):
            every.append(Events(ctx.enter_context(nc.semaphore("a_" + name)), step, ahead))
            return every[-1]

        w_qkv = [[sb(f"w_{n}{h}", [P, NI, D], F32R) for h in range(2)] for n in "qkv"]
        w_ffn = sb("w_ffn", [P, NI, D])
        factors = [sb(f"factors{g}", [2 * RANK, 2 * D]) for g in range(GC)]
        w_sum = sb("w_sum", [P, 2, D])
        w_eff = [[sb(f"w_eff{g}{h}", [P, NI, D], F32R) for h in range(2)] for g in range(GC)]
        x_in = sb("x_in", [P, CT, D])
        x_b = sb("x_b", [P, CT, D])
        w_in = x_b
        x_n = sb("x_n", [P, CT, D])
        x_t = [sb(f"x_t{h}", [P, NI, CH], F32R) for h in range(2)]
        x1 = sb("x1", [P, CT, D])
        x1_b = sb("x1_b", [P, 2, D])
        stats, moments = sb("stats", [P, 2, CT, 6]), sb("moments", [P, 2, CT, 2])
        var_eps, rstd = sb("var_eps", [P, 2, CT]), sb("rstd", [P, 2, CT])
        qk = sb("qk", [P, 2, CH])
        rest = sb("rest", [P, 2, CH])
        parts = sb("parts", [P, 2, PARTS, CH], BF16)
        v_tile = sb("v_tile", [P, 2, HEADS, VC])
        biases = sb("biases", [P, 3, D])
        b_qk = sb("b_qk", [P, 2, NI])

        w_loaded, w_hi, w_cut = events("w_loaded", 16), events("w_hi"), events("w_cut")
        params_in, shared_in = events("params_in", 16 * 6), events("shared_in", 16 * 2 * GC)
        factors_in = [events(f"factors_in{g}", 16) for g in range(GC)]
        consts = events("consts", 3)
        x_loaded, xb_made = events("x_loaded", 16), events("xb_made")
        eff_made, sum_made = events("eff_made"), events("sum_made", ahead=2)
        eff_hi, eff_cut = events("eff_hi"), events("eff_cut", ahead=2)
        st_ok, mom_ok, var_ok, rstd_ok, norm_ok = [[events(f"{s}{n}") for n in range(2)] for s in
                                                   ("st_ok", "mom_ok", "var_ok", "rstd_ok", "norm_ok")]
        turned, t_hi, t_cut = events("turned"), events("t_hi"), events("t_cut", ahead=2)
        ffn_made, ffn_taken = events("ffn_made", ahead=1), events("ffn_taken")
        v_made, v_taken = events("v_made"), events("v_taken")
        v_out = [events(f"v_out{n}", 16, 1) for n in range(2)]
        qk_made, qk_taken = events("qk_made", ahead=1), events("qk_taken", ahead=CT)
        part1, rest_ok, part2, qk_cut = events("part1"), events("rest_ok"), events("part2"), events("qk_cut", ahead=2)
        parts_out = [events(f"parts_out{n}", 16, 1) for n in range(2)]
        x1b_made, x1_out = events("x1b_made", ahead=CT), [events(f"x1_out{n}", 16, 1) for n in range(2)]

        waited = events("waited")

        block = ctx.enter_context(nc.Block())
        x_view = x.rearrange("(t p) d -> p t d", p=P)
        x1_view = x1_scr.rearrange("(t p) d -> p t d", p=P)

        @block.sync
        def _(sp):
            sp.dma_start(x_in[:, :, :], x_view[:, 0:CT, :]).then_inc(x_loaded.sem, 16)
            for b, src in enumerate((bv, bo, ffn_b)):
                sp.dma_start(biases[:, b, :], src).then_inc(params_in.sem, 16)
            sp.dma_start(w_ffn[:, :, :], ffn_w.rearrange("(c p) d -> p c d", p=P)).then_inc(params_in.sem, 16)
            sp.dma_start(b_qk[:, 0, :], bq).then_inc(params_in.sem, 16)
            sp.dma_start(b_qk[:, 1, :], bk).then_inc(params_in.sem, 16)
            for g in range(GC):
                sp.dma_start(factors[g][RANK:2 * RANK, 0:D], lora_as).then_inc(shared_in.sem, 16)
                sp.dma_start(factors[g][RANK:2 * RANK, D:2 * D], lora_bs).then_inc(shared_in.sem, 16)
                sp.dma_start(factors[g][0:RANK, :], lora_scr[g, :, :]).then_inc(factors_in[g].sem, 16)
            for n, w in enumerate((wqT, wkT, wvT)):
                if n:
                    sp.wait_ge(*w_cut[n - 1])
                sp.dma_start(w_in[:, :, :], w.rearrange("(c p) d -> p c d", p=P)).then_inc(w_loaded.sem, 16)

            def chunk(i, last):
                row, half = i // 2, i % 2
                if not last:
                    sp.wait_ge(*norm_ok[0][i * CT + CT - 1])
                    sp.wait_ge(*xb_made[i * CT + CT - 1])
                    sp.dma_start(x_in[:, :, :], x_view[:, bass.ds((i + 1) * CT, CT), :]).then_inc(x_loaded.sem, 16)
                    sp.wait_ge(*eff_made[i * GC * NI + GC * NI - 1])
                    for g in range(GC):
                        src = lora_scr[bass.ds((i + 1) * GC + g, 1), :, :].rearrange("a r d -> (a r) d")
                        sp.dma_start(factors[g][0:RANK, :], src).then_inc(factors_in[g].sem, 16)
                for t in range(CT):
                    sp.wait_ge(*x1b_made[i * CT + t])
                    sp.dma_start(x1_view[:, bass.ds(i * CT + t, 1), :],
                                 x1_b[:, t % 2:t % 2 + 1, :]).then_inc(x1_out[t % 2].sem, 16)
                for t in range(CT):
                    sp.wait_ge(*v_taken[i * CT + t])
                    dst = v_scr[bass.ds(row * NG, NG), bass.ds(half * CH + t * P, P), :].rearrange("g p v -> p g v")
                    src = v_tile[:, t % 2, :, :].rearrange("p (g h) v -> p g (h v)", g=NG)
                    sp.dma_start(dst, src).then_inc(v_out[t % 2].sem, 16)
                for j in range(2 * NI):
                    scr = (q_scr, k_scr)[j // NI]
                    sp.wait_ge(*qk_cut[i * 2 * NI + j])
                    dst = scr[:, bass.ds(row * D + (j % NI) * P, P), bass.ds(half * CH, CH)].rearrange("s p n -> p s n")
                    sp.dma_start(dst, parts[:, j % 2, :, :]).then_inc(parts_out[j % 2].sem, 16)

            with sp.Fori(0, NCH - 1) as i:
                chunk(i, False)
            chunk(NCH - 1, True)
            for n in range(2):
                sp.wait_ge(*x1_out[n][NCH * CT // 2 - 1])
                sp.wait_ge(*v_out[n][NCH * CT // 2 - 1])
                sp.wait_ge(*parts_out[n][NCH * NI - 1])

        @block.gpsimd
        def _(pool):
            give_ahead(pool, every)
            pool.memset(v_tile[:, :, :, HD:VC], 1.0).then_inc(consts.sem, 1)
            pool.wait_ge(*params_in[0])
            pool.tensor_scalar(biases[:, 2, :], biases[:, 2, :], 0.5, None, ALU.mult).then_inc(consts.sem, 1)
            pool.tensor_scalar(b_qk[:, 0, :], b_qk[:, 0, :], float(HD) ** -0.5, None, ALU.mult).then_inc(consts.sem, 1)
            pool.wait_ge(*consts[0])

            def rstd_of(ln, i, t):
                pool.wait_ge(*mom_ok[ln][i * CT + t])
                pool.tensor_tensor(var_eps[:, ln, t:t + 1], moments[:, ln, t, 1:2], eps, ALU.add).then_inc(var_ok[ln].sem, 1)
                pool.wait_ge(*var_ok[ln][i * CT + t])
                pool.tensor_tensor(rstd[:, ln, t:t + 1], var_eps[:, ln, t:t + 1], neg_half,
                                   ALU.pow).then_inc(rstd_ok[ln].sem, 1)

            def add_bias(i):
                pool.wait_ge(*x_loaded[i])
                for t in range(CT):
                    pool.tensor_tensor(x_b[:, t, :], x_in[:, t, :], biases[:, 2, :], ALU.add).then_inc(xb_made.sem, 1)

            def store_x1(i, t):
                pool.wait_ge(*ffn_taken[i * CT + t])
                pool.wait_ge(*x1_out[t % 2][i * (CT // 2) + t // 2 - 1])
                pool.tensor_tensor(x1_b[:, t % 2, :], x1[:, t, :], biases[:, 1, :], ALU.add).then_inc(x1b_made.sem, 1)

            def chunk(i, last):
                for t in range(CT):
                    rstd_of(1, i, t)
                    if t:
                        store_x1(i, t - 1)
                store_x1(i, CT - 1)
                if not last:
                    for t in range(CT):
                        rstd_of(0, i + 1, t)
                    add_bias(i + 1)

            for t in range(CT):
                rstd_of(0, 0, t)
            pool.wait_ge(*w_cut[2])
            add_bias(0)
            with pool.Fori(0, NCH - 1) as i:
                chunk(i, False)
            chunk(NCH - 1, True)

        @block.scalar
        def _(act):
            for n in range(3):
                act.wait_ge(*w_loaded[n])
                act.activation(w_qkv[n][0][:, :, :], w_in[:, :, :], ACT.Copy).then_inc(w_hi.sem, 1)
            act.wait_ge(*consts[0])

            def second_part(i, j):
                act.wait_ge(*rest_ok[i * 2 * NI + j])
                act.activation(parts[:, j % 2, 1, :], rest[:, j % 2, :], ACT.Copy).then_inc(part2.sem, 1)

            def chunk(i):
                act.wait_ge(*ffn_made[i * CT - 1])
                for n in range(GC * NI):
                    act.wait_ge(*sum_made[i * GC * NI + n])
                    act.activation(w_eff[n // NI][0][:, n % NI, :], w_sum[:, n % 2, :], ACT.Copy).then_inc(eff_hi.sem, 1)
                act.wait_ge(*qk_made[i * 2 * NI - 1])
                for n in range(2 * CT):
                    act.wait_ge(*turned[i * 2 * CT + n])
                    if n >= CT:
                        act.wait_ge(*ffn_made[i * CT + n - CT])
                    at = n % CT * P
                    act.activation(x_t[0][:, :, at:at + P], ps[:, 2 + n % 2, :].rearrange("p (c n) -> p c n", c=NI),
                                   ACT.Copy).then_inc(t_hi.sem, 1)
                for j in range(2 * NI):
                    kq, n = j // NI, i * 2 * NI + j
                    act.wait_ge(*qk_made[n])
                    act.wait_ge(*qk_cut[n - 2])
                    act.activation(qk[:, j % 2, :], ps[:, 4 + j % 4, :], ACT.Identity,
                                   bias=b_qk[:, kq, j % NI:j % NI + 1],
                                   scale=(float(HD) ** -0.5, 1.0)[kq]).then_inc(qk_taken.sem, 1)
                    act.wait_ge(*qk_taken[n])
                    act.wait_ge(*parts_out[j % 2][i * NI + j // 2 - 1])
                    act.activation(parts[:, j % 2, 0, :], qk[:, j % 2, :], ACT.Copy).then_inc(part1.sem, 1)
                    if j:
                        second_part(i, j - 1)
                second_part(i, 2 * NI - 1)

            with act.Fori(0, NCH) as i:
                chunk(i)

        @block.vector
        def _(dve):
            def norm(ln, i, t, rows):
                dve.bn_stats(stats[:, ln, t, :], rows).then_inc(st_ok[ln].sem, 1)
                dve.wait_ge(*st_ok[ln][i * CT + t])
                dve.sem_inc(waited.sem, 1)
                dve.bn_aggr(moments[:, ln, t, :], stats[:, ln, t, :]).then_inc(mom_ok[ln].sem, 1)

            def norm_out(ln, i, t, rows):
                dve.wait_ge(*rstd_ok[ln][i * CT + t])
                dve.tensor_scalar(x_n[:, t, :], rows, moments[:, ln, t, 0:1], rstd[:, ln, t:t + 1],
                                  ALU.subtract, ALU.mult).then_inc(norm_ok[ln].sem, 1)

            def turn_lo(i, n):
                dve.wait_ge(*t_hi[i * 2 * CT + n])
                at = n % CT * P
                dve.tensor_tensor(x_t[1][:, :, at:at + P], ps[:, 2 + n % 2, :].rearrange("p (c n) -> p c n", c=NI),
                                  x_t[0][:, :, at:at + P].bitcast(F32), ALU.subtract).then_inc(t_cut.sem, 1)

            def sum_lo(i, n):
                dve.wait_ge(*eff_hi[i * GC * NI + n])
                dve.tensor_tensor(w_eff[n // NI][1][:, n % NI, :], w_sum[:, n % 2, :],
                                  w_eff[n // NI][0][:, n % NI, :].bitcast(F32), ALU.subtract).then_inc(eff_cut.sem, 1)

            def third_part(i, j):
                dve.wait_ge(*part2[i * 2 * NI + j])
                dve.tensor_tensor(parts[:, j % 2, 2, :], rest[:, j % 2, :], parts[:, j % 2, 1, :],
                                  ALU.subtract).then_inc(qk_cut.sem, 1)

            def ffn_sum(i, t):
                dve.wait_ge(*ffn_made[i * CT + t])
                dve.wait_ge(*xb_made[i * CT + t])
                dve.wait_ge(*x1b_made[i * CT + t - CT])
                dve.scalar_tensor_tensor(out=x1[:, t, :], in0=ps[:, 4 + t, :], scalar=0.5, in1=x_b[:, t, :],
                                         op0=ALU.mult, op1=ALU.add).then_inc(ffn_taken.sem, 1)
                dve.wait_ge(*ffn_taken[i * CT + t])
                norm(1, i, t, x1[:, t, :])

            def v_sum(i, t):
                dve.wait_ge(*v_made[i * CT + t])
                dve.wait_ge(*v_out[t % 2][i * (CT // 2) + t // 2 - 1])
                dve.tensor_tensor(v_tile[:, t % 2, :, 0:HD], ps[:, 4 + t, :].rearrange("p (h d) -> p h d", h=HEADS),
                                  biases[:, 0, :].rearrange("p (h d) -> p h d", h=HEADS), ALU.add).then_inc(v_taken.sem, 1)

            def chunk(i, last):
                for n in range(GC * NI):
                    dve.wait_ge(*eff_made[i * GC * NI + n])
                    dve.wait_ge(*eff_cut[i * GC * NI + n - 2])
                    dve.tensor_tensor(w_sum[:, n % 2, :], ps[:, n % 2, :], w_ffn[:, n % NI, :],
                                      ALU.add).then_inc(sum_made.sem, 1)
                    if n:
                        sum_lo(i, n - 1)
                sum_lo(i, GC * NI - 1)
                for t in range(CT):
                    turn_lo(i, t)
                for t in range(CT):
                    ffn_sum(i, t)
                    norm_out(1, i, t, x1[:, t, :])
                    if t:
                        turn_lo(i, CT + t - 1)
                    if t > 1:
                        v_sum(i, t - 2)
                v_sum(i, CT - 2)
                turn_lo(i, 2 * CT - 1)
                v_sum(i, CT - 1)
                if not last:
                    dve.wait_ge(*x_loaded[i + 1])
                for j in range(2 * NI):
                    dve.wait_ge(*part1[i * 2 * NI + j])
                    dve.tensor_tensor(rest[:, j % 2, :], qk[:, j % 2, :], parts[:, j % 2, 0, :],
                                      ALU.subtract).then_inc(rest_ok.sem, 1)
                    if j:
                        third_part(i, j - 1)
                    if not last and j < CT:
                        norm(0, i + 1, j, x_in[:, j, :])
                    if not last and 2 <= j < CT + 2:
                        norm_out(0, i + 1, j - 2, x_in[:, j - 2, :])
                third_part(i, 2 * NI - 1)

            dve.wait_ge(*x_loaded[0])
            for t in range(CT):
                norm(0, 0, t, x_in[:, t, :])
            for t in range(CT):
                norm_out(0, 0, t, x_in[:, t, :])
            for n in range(3):
                dve.wait_ge(*w_hi[n])
                dve.tensor_tensor(w_qkv[n][1][:, :, :], w_in[:, :, :], w_qkv[n][0][:, :, :].bitcast(F32),
                                  ALU.subtract).then_inc(w_cut.sem, 1)
            dve.wait_ge(*consts[0])
            dve.wait_ge(*params_in[0])
            with dve.Fori(0, NCH - 1) as i:
                chunk(i, False)
            chunk(NCH - 1, True)

        @block.tensor
        def _(pe):
            pe.wait_ge(*shared_in[0])
            pe.wait_ge(*w_cut[2])

            def turn(i, n):
                ln, t = n // CT, n % CT
                pe.wait_ge(*norm_ok[ln][i * CT + t])
                pe.wait_ge(*t_cut[i * 2 * CT + n - 2])
                for ic in range(NI):
                    mm = pe.transpose(ps[:, 2 + n % 2, ic * P:(ic + 1) * P], x_n[:, t, ic * P:(ic + 1) * P], ident[:, :])
                mm.then_inc(turned.sem, 1)

            def rows(t):
                return lambda h, ic: x_t[h][:, ic, t * P:(t + 1) * P]

            def ffn(i, t):
                pe.wait_ge(*t_cut[i * 2 * CT + t])
                pe.wait_ge(*eff_cut[i * GC * NI + (t // GT + 1) * NI - 1])
                pe.wait_ge(*qk_taken[i * 2 * NI - CT + t])
                project(pe, ps[:, 4 + t, :], rows(t), lambda h, ic: w_eff[t // GT][h][:, ic, :], ffn_made.sem)

            def v_rows(i, t):
                pe.wait_ge(*t_cut[i * 2 * CT + CT + t])
                pe.wait_ge(*ffn_taken[i * CT + t])
                project(pe, ps[:, 4 + t, :], rows(t), lambda h, ic: w_qkv[2][h][:, ic, :], v_made.sem)

            def chunk(i):
                for g in range(GC):
                    pe.wait_ge(*factors_in[g][i])
                    for ic in range(NI):
                        n = g * NI + ic
                        pe.wait_ge(*sum_made[i * GC * NI + n - 2])
                        pe.matmul(ps[:, n % 2, :], factors[g][:, ic * P:(ic + 1) * P], factors[g][:, D:2 * D],
                                  start=True, stop=True).then_inc(eff_made.sem, 1)
                for t in range(CT):
                    turn(i, t)
                for t in range(CT):
                    ffn(i, t)
                    if t >= 2:
                        turn(i, CT + t - 2)
                v_rows(i, 0)
                turn(i, 2 * CT - 2)
                v_rows(i, 1)
                v_rows(i, 2)
                turn(i, 2 * CT - 1)
                v_rows(i, 3)
                for j in range(2 * NI):
                    at = j % NI * P
                    if j < CT:
                        pe.wait_ge(*v_taken[i * CT + j])
                    else:
                        pe.wait_ge(*qk_taken[i * 2 * NI + j - CT])
                    project(pe, ps[:, 4 + j % 4, :], lambda h, ic: w_qkv[j // NI][h][:, ic, at:at + P],
                            lambda h, ic: x_t[h][:, ic, :], qk_made.sem)

            with pe.Fori(0, NCH) as i:
                chunk(i)


def score_jobs():
    first = [("max", 0, h, q, 0, (q + 1) * P) for q in range(CT) for h in range(HG)]
    second = []
    for q in range(CT):
        for h in range(HG):
            second += [("max", 1, h, q, 0, CH), ("max", 1, h, q, CH, (q + 1) * P)]
    return first, second


def stage_b(nc, ps, ident, causal, q_scr, k_scr, v_scr, o_scr):
    with ExitStack() as ctx:
        every = []

        def sb(name, shape, dt=F32):
            return ctx.enter_context(nc.sbuf_tensor("b_" + name, shape, dt))

        def events(name, step=1, ahead=0):
            every.append(Events(ctx.enter_context(nc.semaphore("b_" + name)), step, ahead))
            return every[-1]

        S_BANK, O_BANK, RING, NRING = 0, 4, 5, 3
        AHEAD = 2

        q_pack = [sb(f"q_pack{n}", [SROWS, 2, HG, CH], BF16) for n in range(NPACK)]
        k_pack = [sb(f"k_pack{n}", [SROWS, HG, SEQ], BF16) for n in range(NPACK)]
        v_pack = [sb(f"v_pack{n}", [P, QT, HG * VC]) for n in range(NPACK)]
        probs = sb("probs", [P, PBUF, HG, CH])
        top = sb("top", [P, 4, HG * CT])
        neg_top = sb("neg_top", [HG * CT, 2, 2, P], BF16)
        o_t = sb("o_t", [P, 2, CH])
        inv = sb("inv", [P, 2, HG * CT])
        o_rows = sb("o_rows", [P, 2, HG * CT, HD])

        def width(s):
            c, kt = STEPS[s]
            return CH - max(0, kt - CT * c) * P

        first, second = score_jobs()
        ring_start = first + [("turn", 0)] + second
        J0 = len(ring_start)

        def jobs_by_step():
            todo = first + [("turn", 0)] + second
            cost = [75 + (job[5] if job[0] == "max" else P) for job in todo]
            all_cost, all_width = sum(cost), sum(map(width, range(NS)))
            by_step, given = [], 0.0
            for s in range(NS):
                now = [("turn", 1)] if s == 0 else []
                goal = all_cost * sum(map(width, range(s + 1))) / all_width
                while todo and given + cost[0] / 2 <= goal:
                    now.append(todo.pop(0))
                    given += cost.pop(0)
                if s == CT + OUT_LAG:
                    now.append(("out", 0))
                by_step.append(now)
            return by_step[:-1] + [by_step[-1] + todo + [("out", 1)]]

        OUT_LAG = 0
        by_step = jobs_by_step()
        ring = sum(by_step, [])
        J = len(ring)
        tail = [[("turn", 1)] if s == 0 else [("out", 0)] if s == CT + OUT_LAG else [("out", 1)] if s == NS - 1 else []
                for s in range(NS)]

        EMPTY = (20, 36)
        slot = [n + sum(n >= e for e in EMPTY) for n in range(J)]
        SLOTS = J + len(EMPTY)
        SHIFT = -J0 % NRING
        assert SLOTS % NRING == 0

        def bank(n):
            return RING + slot[n] % NRING

        def earlier(n):
            s = slot[n]
            while True:
                s -= NRING
                if s < 0:
                    return slot.index(s + SLOTS) - J
                if s in slot:
                    return slot.index(s)

        def ring_of(more):
            return ring if more else sum(tail, [])

        loaded = [events(f"loaded{n}", 16 * LOADS) for n in range(NPACK)]
        ones_ok = events("ones_ok", NPACK * 2 + 1)
        ring_made, ring_taken = events("ring_made"), events("ring_taken", ahead=NRING)
        top_ok, neg_hi = events("top_ok"), events("neg_hi")
        neg_in = [events(f"neg_in{c}", 32, 1) for c in range(2)]
        s_made, s_taken = events("s_made"), events("s_taken", ahead=2)
        masked = events("masked")
        pv_made = events("pv_made", ahead=PBUF)
        o_taken = events("o_taken", ahead=1)
        inv_ok = events("inv_ok")
        o_out = [events(f"o_out{c}", 16, 1) for c in range(2)]

        waited = events("waited")

        block = ctx.enter_context(nc.Block())

        TRIPLES = (UNITS - 2) // NPACK

        def over_units(eng, unit):
            with eng.Fori(0, TRIPLES) as i:
                for r in range(NPACK):
                    unit(i * NPACK + r, r, i, True, True)
            for u in range(TRIPLES * NPACK, UNITS):
                unit(u, u % NPACK, u // NPACK, u + 1 < UNITS, u + 2 < UNITS)

        @block.sync
        def _(sp):
            def load(u, r):
                rows = HG * HD
                for n, (q_part, k_part) in enumerate(TERMS):
                    at = slice(n * HD, (n + 1) * HD)
                    for c in range(2):
                        src = q_scr[q_part, bass.ds(u * rows, rows), c * CH:(c + 1) * CH].rearrange("(h d) n -> d h n", h=HG)
                        sp.dma_start(q_pack[r][at, c, :, :], src).then_inc(loaded[r].sem, 16)
                    src = k_scr[k_part, bass.ds(u * rows, rows), :].rearrange("(h d) n -> d h n", h=HG)
                    sp.dma_start(k_pack[r][at, :, :], src).then_inc(loaded[r].sem, 16)
                src = v_scr[bass.ds(u, 1), :, :].rearrange("a (t p) v -> p (a t) v", p=P)
                sp.dma_start(v_pack[r][:, :, :], src).then_inc(loaded[r].sem, 16)

            def neg_rows(u, r, c, taken):
                sp.wait_ge(*taken)
                for part in range(2):
                    sp.dma_start(q_pack[r][KROWS + part:KROWS + part + 1, c, :, :].rearrange("a h n -> a (h n)"),
                                 neg_top[:, c, part, :]).then_inc(neg_in[c].sem, 16)

            def store(u, c, taken):
                sp.wait_ge(*taken)
                dst = o_scr[bass.ds(u, 1), c * CH:(c + 1) * CH, :].rearrange("a (t p) v -> p (a t) v", p=P)
                sp.dma_start(dst, o_rows[:, c, :, :].rearrange("p (t h) d -> p t (h d)", t=CT)).then_inc(o_out[c].sem, 16)

            def unit(u, r, i, more, more2):
                neg_rows(u, r, 1, ring_taken[u * J + (J0 + ring.index(("turn", 1)))])
                if more2:
                    sp.wait_ge(*pv_made[u * NS - 1])
                    load(u + 2, (r + 2) % NPACK)
                outs = [n for n, job in enumerate(ring_of(more)) if job[0] == "out"]
                store(u, 0, ring_taken[u * J + (J0 + outs[0])])
                if more:
                    neg_rows(u + 1, (r + 1) % NPACK, 0, ring_taken[u * J + (J0 + ring.index(("turn", 0)))])
                store(u, 1, ring_taken[u * J + (J0 + outs[1])])

            load(0, 0)
            load(1, 1)
            neg_rows(0, 0, 0, ring_taken[len(first)])
            over_units(sp, unit)
            for c in range(2):
                sp.wait_ge(*o_out[c][UNITS - 1])

        @block.gpsimd
        def _(pool):
            give_ahead(pool, every)
            for n in range(NPACK):
                pool.memset(k_pack[n][KROWS:SROWS, :, :], 1.0).then_inc(ones_ok.sem, 1)

            def unit(u, r, i, more, more2):
                for s in DIAG:
                    pool.wait_ge(*s_taken[u * 2 * NS + 2 * s + 1])
                    pool.sem_inc(waited.sem, 1)
                    block_ = probs[:, s % PBUF, :, 0:P]
                    pool.affine_select(out=block_, in_=block_, compare_op=ALU.is_ge, fill=0.0, base=0,
                                       pattern=[[0, HG], [1, P]], channel_multiplier=-1).then_inc(masked.sem, 1)

            with pool.Fori(0, UNITS) as u:
                unit(u, None, None, None, None)

        @block.scalar
        def _(act):
            def exps(u, s):
                c, kt = STEPS[s]
                width = CH - max(0, kt - CT * c) * P
                act.wait_ge(*pv_made[u * NS + s - PBUF])
                for half in range(2):
                    act.wait_ge(*s_made[u * 2 * NS + 2 * s + half])
                    act.activation(probs[:, s % PBUF, 2 * half:2 * half + 2, 0:width],
                                   ps[:, S_BANK + 2 * half:S_BANK + 2 * half + 2, 0:width], ACT.Exp).then_inc(s_taken.sem, 1)

            def take_out(u, c):
                last = [n for n, (cc, _) in enumerate(STEPS) if cc == c][-1]
                act.wait_ge(*pv_made[u * NS + last])
                act.activation(o_t[:, c, :], ps[:, O_BANK, :], ACT.Copy).then_inc(o_taken.sem, 1)

            def unit(u, more):
                for s in range(1, NS):
                    exps(u, s)
                    if s == CT:
                        take_out(u, 0)
                if more:
                    exps(u + 1, 0)
                take_out(u, 1)

            act.wait_ge(*ones_ok[0])
            exps(0, 0)
            with act.Fori(0, UNITS - 1) as u:
                unit(u, True)
            unit(UNITS - 1, False)

        @block.vector
        def _(dve):
            dve.memset(ps[:, O_BANK, :], 0.0).then_inc(ones_ok.sem, 1)
            for n in range(NPACK):
                dve.memset(q_pack[n][KROWS:SROWS, :, :, :], 0.0).then_inc(ones_ok.sem, 1)

            def job(what, n, n_bank, u):
                dve.wait_ge(*ring_made[n])
                if what[0] == "max":
                    _, c, h, q, a, w = what
                    at = h * CT + q
                    if a == 0 and w == CH and c == 1:
                        dve.tensor_reduce(top[:, 1, at:at + 1], ps[:, n_bank, :], AX.X, ALU.max).then_inc(ring_taken.sem, 1)
                    else:
                        dve.sem_inc(waited.sem, 1)
                        dve.tensor_tensor_reduce(ps[:, n_bank, 0:w], ps[:, n_bank, 0:w], causal[:, CH - w:CH], 1.0, FMIN,
                                                 ALU.add, ALU.max, top[:, 2 * c, at:at + 1]).then_inc(ring_taken.sem, 1)
                elif what[0] == "turn":
                    c = what[1]
                    dve.wait_ge(*neg_in[c][(u + (1 - c)) - 1])
                    dve.tensor_scalar(neg_top[:, c, 0, :], ps[0:HG * CT, n_bank, 0:P], -1.0, None,
                                      ALU.mult).then_inc(neg_hi.sem, 1)
                    dve.wait_ge(*neg_hi[u * 2 + (2 - c)])
                    dve.scalar_tensor_tensor(out=neg_top[:, c, 1, :], in0=ps[0:HG * CT, n_bank, 0:P], scalar=-1.0,
                                             in1=neg_top[:, c, 0, :], op0=ALU.mult,
                                             op1=ALU.subtract).then_inc(ring_taken.sem, 1)
                else:
                    c = what[1]
                    banks = ps[:, n_bank, :].rearrange("p (n v) -> p n v", v=32)
                    dve.reciprocal(inv[:, c, :].unsqueeze(2), banks[:, :, HD:VC]).then_inc(inv_ok.sem, 1)
                    dve.wait_ge(*inv_ok[u * 2 + c])
                    dve.wait_ge(*o_out[c][u - 1])
                    dve.tensor_tensor(o_rows[:, c, :, :], banks[:, :, 0:HD],
                                      inv[:, c, :].unsqueeze(2).to_broadcast([P, HG * CT, HD]),
                                      ALU.mult).then_inc(ring_taken.sem, 1)

            def join_top(u, n):
                dve.wait_ge(*ring_taken[n])
                dve.tensor_tensor(top[:, 3, :], top[:, 1, :], top[:, 2, :], ALU.max).then_inc(top_ok.sem, 1)

            for n, what in enumerate(ring_start):
                job(what, n, RING + (n + SHIFT) % NRING, -1)
            join_top(0, J0 - 1)

            def unit(u, r, i, more, more2):
                for n, what in enumerate(ring_of(more)):
                    job(what, u * J + (J0 + n), bank(n), u)
                    if what == second[-1]:
                        join_top(u + 1, u * J + (J0 + n))

            with dve.Fori(0, UNITS - 1) as u:
                unit(u, None, None, True, True)
            unit(UNITS - 1, None, None, False, False)

        @block.tensor
        def _(pe):
            def job(what, n, n_bank, free, r, u, half0):
                pe.wait_ge(*ring_taken[free])
                if what[0] == "max":
                    _, c, h, q, a, w = what
                    mm = pe.matmul(ps[:, n_bank, 0:w], q_pack[r][0:KROWS, c, h, q * P:(q + 1) * P], k_pack[r][0:KROWS, h, a:a + w],
                                   start=True, stop=True)
                elif what[0] == "turn":
                    c = what[1]
                    if c == 0:
                        pe.wait_ge(*ring_taken[half0])
                    else:
                        pe.wait_ge(*top_ok[u])
                    mm = pe.transpose(ps[0:HG * CT, n_bank, 0:P], top[:, 3 * c, :], ident[:, :])
                else:
                    c = what[1]
                    pe.wait_ge(*o_taken[u * 2 + c])
                    for q in range(CT):
                        mm = pe.transpose(ps[:, n_bank, q * P:(q + 1) * P], o_t[:, c, q * P:(q + 1) * P], ident[:, :])
                mm.then_inc(ring_made.sem, 1)

            def scores(u, r, s, half):
                c, kt = STEPS[s]
                skip = max(0, kt - CT * c) * P
                if half == 0 and (s == 0 or STEPS[s - 1][0] != c):
                    pe.wait_ge(*neg_in[c][u])
                pe.wait_ge(*s_taken[u * 2 * NS + 2 * s + half - 2])
                for h in range(2 * half, 2 * half + 2):
                    mm = pe.matmul(ps[:, S_BANK + h, 0:CH - skip], k_pack[r][:, h, kt * P:(kt + 1) * P],
                                   q_pack[r][:, c, h, skip:CH], start=True, stop=True)
                mm.then_inc(s_made.sem, 1)

            def values(u, r, s):
                c, kt = STEPS[s]
                skip = max(0, kt - CT * c) * P
                if s in DIAG:
                    pe.wait_ge(*masked[u * len(DIAG) + DIAG.index(s)])
                else:
                    pe.wait_ge(*s_taken[u * 2 * NS + 2 * s + 1])
                if kt == 0:
                    pe.wait_ge(*o_taken[u * 2 + c - 1])
                for h in range(HG):
                    mm = pe.matmul(ps[32 * h:32 * h + VC, O_BANK, skip:CH], v_pack[r][:, kt, h * VC:(h + 1) * VC],
                                   probs[:, s % PBUF, h, 0:CH - skip], start=(kt == 0),
                                   stop=(kt == CT * (c + 1) - 1))
                mm.then_inc(pv_made.sem, 1)

            pe.wait_ge(*ones_ok[0])
            pe.wait_ge(*loaded[0][0])
            for n, what in enumerate(ring_start):
                job(what, n, RING + (n + SHIFT) % NRING, n - NRING, 0, -1, len(first) - 1)
            for s in range(AHEAD):
                scores(0, 0, s, 0)
                scores(0, 0, s, 1)

            def unit(u, r, i, more, more2):
                if more:
                    nr, ni = (r + 1) % NPACK, i + (r + 1) // NPACK
                    pe.wait_ge(*loaded[nr][ni])
                n = 0
                for s in range(NS):
                    jobs = (by_step if more else tail)[s]
                    for place in range(3):
                        if place != 1 and s + AHEAD < NS:
                            scores(u, r, s + AHEAD, place // 2)
                        elif place != 1 and more:
                            scores(u + 1, (r + 1) % NPACK, s + AHEAD - NS, place // 2)
                        elif place == 1:
                            values(u, r, s)
                        for what in jobs[len(jobs) * place // 3:len(jobs) * (place + 1) // 3]:
                            job(what, u * J + (J0 + n), bank(n), u * J + (J0 + earlier(n)), (r + 1) % NPACK, u,
                                u * J + (J0 + len(first)))
                            n += 1

            over_units(pe, unit)


def stage_c(nc, ps, ident, neg_half, eps, woT, ffn_w, ffn_b, lora_as, lora_bs, lora_scr, x1_scr, o_scr, out):
    with ExitStack() as ctx:
        every = []

        def sb(name, shape, dt=F32):
            return ctx.enter_context(nc.sbuf_tensor("c_" + name, shape, dt))

        def events(name, step=1, ahead=0):
            every.append(Events(ctx.enter_context(nc.semaphore("c_" + name)), step, ahead))
            return every[-1]

        w_out = [sb(f"w_out{h}", [P, NI, D], F32R) for h in range(2)]
        w_ffn = sb("w_ffn", [P, NI, D])
        w_in = sb("w_in", [P, NI, D])
        factors = [sb(f"factors{g}", [2 * RANK, 2 * D]) for g in range(GC)]
        w_sum = sb("w_sum", [P, 2, D])
        w_eff = [[sb(f"w_eff{g}{h}", [P, NI, D], F32R) for h in range(2)] for g in range(GC)]
        o_in = sb("o_in", [P, CT, D])
        x1_in = sb("x1_in", [P, CT, D])
        x2 = sb("x2", [P, CT, D])
        x2_b = sb("x2_b", [P, CT, D])
        x_n = sb("x_n", [P, CT, D])
        x_t = [[sb(f"x_t{n}{h}", [P, NI, CH], F32R) for h in range(2)] for n in range(2)]
        y = sb("y", [P, 2, D])
        bias = sb("bias", [P, D])
        stats, moments = sb("stats", [P, CT, 6]), sb("moments", [P, CT, 2])
        var_eps, rstd = sb("var_eps", [P, CT]), sb("rstd", [P, CT])

        w_loaded, w_hi, w_cut = events("w_loaded", 16), events("w_hi"), events("w_cut")
        params_in, shared_in = events("params_in", 16 * 2), events("shared_in", 16 * 2 * GC)
        factors_in = [events(f"factors_in{g}", 16) for g in range(GC)]
        bias_ok = events("bias_ok")
        o_loaded, x1_loaded = events("o_loaded", 16 * CT), events("x1_loaded", 16)
        eff_made, sum_made = events("eff_made"), events("sum_made", ahead=2)
        eff_hi, eff_cut = events("eff_hi"), events("eff_cut", ahead=2)
        st_ok, mom_ok, var_ok, rstd_ok, norm_ok = [events(s) for s in ("st_ok", "mom_ok", "var_ok", "rstd_ok", "norm_ok")]
        turned, t_hi, t_cut = events("turned"), events("t_hi"), events("t_cut", ahead=2)
        proj_made, proj_taken = events("proj_made", ahead=1), events("proj_taken")
        x2b_made = events("x2b_made")
        ffn_made, ffn_taken = events("ffn_made", ahead=1), events("ffn_taken", ahead=CT)
        y_out = [events(f"y_out{n}", 16, 1) for n in range(2)]

        waited = events("waited")

        block = ctx.enter_context(nc.Block())
        x1_view = x1_scr.rearrange("(t p) d -> p t d", p=P)
        out_view = out.rearrange("(t p) d -> p t d", p=P)

        @block.sync
        def _(sp):
            def load(i, row, half):
                for t in range(CT):
                    src = o_scr[bass.ds(row * NG, NG), bass.ds(half * CH + t * P, P), :].rearrange("g p v -> p g v")
                    sp.dma_start(o_in[:, t, :].rearrange("p (g v) -> p g v", g=NG), src).then_inc(o_loaded.sem, 16)

            load(0, 0, 0)
            sp.dma_start(w_in[:, :, :], woT.rearrange("(c p) d -> p c d", p=P)).then_inc(w_loaded.sem, 16)
            sp.dma_start(x1_in[:, :, :], x1_view[:, 0:CT, :]).then_inc(x1_loaded.sem, 16)
            for g in range(GC):
                sp.dma_start(factors[g][RANK:2 * RANK, 0:D], lora_as).then_inc(shared_in.sem, 16)
                sp.dma_start(factors[g][RANK:2 * RANK, D:2 * D], lora_bs).then_inc(shared_in.sem, 16)
                sp.dma_start(factors[g][0:RANK, :], lora_scr[g, :, :]).then_inc(factors_in[g].sem, 16)
            sp.dma_start(w_ffn[:, :, :], ffn_w.rearrange("(c p) d -> p c d", p=P)).then_inc(params_in.sem, 16)
            sp.dma_start(bias[:, :], ffn_b).then_inc(params_in.sem, 16)

            def chunk(i, last):
                if not last:
                    sp.wait_ge(*eff_made[i * GC * NI + GC * NI - 1])
                    for g in range(GC):
                        src = lora_scr[bass.ds((i + 1) * GC + g, 1), :, :].rearrange("a r d -> (a r) d")
                        sp.dma_start(factors[g][0:RANK, :], src).then_inc(factors_in[g].sem, 16)
                    sp.wait_ge(*turned[i * 2 * CT + CT - 1])
                    load(i + 1, (i + 1) // 2, (i + 1) % 2)
                    sp.wait_ge(*proj_taken[i * CT + CT - 1])
                    sp.dma_start(x1_in[:, :, :], x1_view[:, bass.ds((i + 1) * CT, CT), :]).then_inc(x1_loaded.sem, 16)
                for t in range(CT):
                    sp.wait_ge(*ffn_taken[i * CT + t])
                    sp.dma_start(out_view[:, bass.ds(i * CT + t, 1), :], y[:, t % 2:t % 2 + 1, :]).then_inc(y_out[t % 2].sem, 16)

            with sp.Fori(0, NCH - 1) as i:
                chunk(i, False)
            chunk(NCH - 1, True)
            for n in range(2):
                sp.wait_ge(*y_out[n][NCH * CT // 2 - 1])

        @block.gpsimd
        def _(pool):
            give_ahead(pool, every)
            pool.wait_ge(*params_in[0])
            pool.tensor_scalar(bias[:, :], bias[:, :], 0.5, None, ALU.mult).then_inc(bias_ok.sem, 1)
            pool.wait_ge(*bias_ok[0])
            with pool.Fori(0, NCH) as i:
                for t in range(CT):
                    pool.wait_ge(*mom_ok[i * CT + t])
                    pool.tensor_tensor(var_eps[:, t:t + 1], moments[:, t, 1:2], eps, ALU.add).then_inc(var_ok.sem, 1)
                    pool.wait_ge(*var_ok[i * CT + t])
                    pool.tensor_tensor(rstd[:, t:t + 1], var_eps[:, t:t + 1], neg_half, ALU.pow).then_inc(rstd_ok.sem, 1)
                    pool.wait_ge(*ffn_taken[i * CT + t - CT])
                    pool.tensor_tensor(x2_b[:, t, :], x2[:, t, :], bias[:, :], ALU.add).then_inc(x2b_made.sem, 1)

        @block.scalar
        def _(act):
            act.wait_ge(*w_loaded[0])
            act.activation(w_out[0][:, :, :], w_in[:, :, :], ACT.Copy).then_inc(w_hi.sem, 1)

            def turn_hi(i, n):
                act.wait_ge(*turned[i * 2 * CT + n])
                at = n % CT * P
                act.activation(x_t[n // CT][0][:, :, at:at + P], ps[:, 2 + n % 2, :].rearrange("p (c n) -> p c n", c=NI),
                               ACT.Copy).then_inc(t_hi.sem, 1)

            with act.Fori(0, NCH) as i:
                act.wait_ge(*proj_made[i * CT - 1])
                act.wait_ge(*ffn_made[i * CT - 1])
                for n in range(GC * NI):
                    act.wait_ge(*sum_made[i * GC * NI + n])
                    act.activation(w_eff[n // NI][0][:, n % NI, :], w_sum[:, n % 2, :], ACT.Copy).then_inc(eff_hi.sem, 1)
                for n in range(2 * CT):
                    turn_hi(i, n)

        @block.vector
        def _(dve):
            def turn_lo(i, n):
                dve.wait_ge(*t_hi[i * 2 * CT + n])
                at = n % CT * P
                dve.tensor_tensor(x_t[n // CT][1][:, :, at:at + P], ps[:, 2 + n % 2, :].rearrange("p (c n) -> p c n", c=NI),
                                  x_t[n // CT][0][:, :, at:at + P].bitcast(F32), ALU.subtract).then_inc(t_cut.sem, 1)

            def sum_lo(i, n):
                dve.wait_ge(*eff_hi[i * GC * NI + n])
                dve.tensor_tensor(w_eff[n // NI][1][:, n % NI, :], w_sum[:, n % 2, :],
                                  w_eff[n // NI][0][:, n % NI, :].bitcast(F32), ALU.subtract).then_inc(eff_cut.sem, 1)

            def take_ffn(i, t):
                dve.wait_ge(*ffn_made[i * CT + t])
                dve.wait_ge(*x2b_made[i * CT + t])
                dve.wait_ge(*y_out[t % 2][i * (CT // 2) + t // 2 - 1])
                dve.scalar_tensor_tensor(out=y[:, t % 2, :], in0=ps[:, 4 + t, :], scalar=0.5, in1=x2_b[:, t, :],
                                         op0=ALU.mult, op1=ALU.add).then_inc(ffn_taken.sem, 1)

            dve.wait_ge(*w_hi[0])
            dve.tensor_tensor(w_out[1][:, :, :], w_in[:, :, :], w_out[0][:, :, :].bitcast(F32),
                              ALU.subtract).then_inc(w_cut.sem, 1)
            dve.wait_ge(*params_in[0])
            with dve.Fori(0, NCH) as i:
                for n in range(GC * NI):
                    dve.wait_ge(*eff_made[i * GC * NI + n])
                    dve.wait_ge(*eff_cut[i * GC * NI + n - 2])
                    dve.tensor_tensor(w_sum[:, n % 2, :], ps[:, n % 2, :], w_ffn[:, n % NI, :],
                                      ALU.add).then_inc(sum_made.sem, 1)
                    if n:
                        sum_lo(i, n - 1)
                sum_lo(i, GC * NI - 1)
                for t in range(CT):
                    turn_lo(i, t)
                dve.wait_ge(*x1_loaded[i])
                for t in range(CT):
                    dve.wait_ge(*proj_made[i * CT + t])
                    dve.tensor_tensor(x2[:, t, :], ps[:, 4 + t, :], x1_in[:, t, :], ALU.add).then_inc(proj_taken.sem, 1)
                    dve.wait_ge(*proj_taken[i * CT + t])
                    dve.bn_stats(stats[:, t, :], x2[:, t, :]).then_inc(st_ok.sem, 1)
                    dve.wait_ge(*st_ok[i * CT + t])
                    dve.sem_inc(waited.sem, 1)
                    dve.bn_aggr(moments[:, t, :], stats[:, t, :]).then_inc(mom_ok.sem, 1)
                    dve.wait_ge(*rstd_ok[i * CT + t])
                    dve.tensor_scalar(x_n[:, t, :], x2[:, t, :], moments[:, t, 0:1], rstd[:, t:t + 1],
                                      ALU.subtract, ALU.mult).then_inc(norm_ok.sem, 1)
                    if t:
                        turn_lo(i, CT + t - 1)
                turn_lo(i, 2 * CT - 1)
                for t in range(CT):
                    take_ffn(i, t)

        @block.tensor
        def _(pe):
            pe.wait_ge(*shared_in[0])

            def turn(i, n, source):
                pe.wait_ge(*t_cut[i * 2 * CT + n - 2])
                t = n % CT
                for ic in range(NI):
                    mm = pe.transpose(ps[:, 2 + n % 2, ic * P:(ic + 1) * P], source[:, t, ic * P:(ic + 1) * P], ident[:, :])
                mm.then_inc(turned.sem, 1)

            def ffn(i, t):
                pe.wait_ge(*t_cut[i * 2 * CT + CT + t])
                pe.wait_ge(*eff_cut[i * GC * NI + (t // GT + 1) * NI - 1])
                pe.wait_ge(*proj_taken[i * CT + t])
                project(pe, ps[:, 4 + t, :], lambda h, ic: x_t[1][h][:, ic, t * P:(t + 1) * P],
                        lambda h, ic: w_eff[t // GT][h][:, ic, :], ffn_made.sem)

            with pe.Fori(0, NCH) as i:
                for g in range(GC):
                    pe.wait_ge(*factors_in[g][i])
                    for ic in range(NI):
                        n = g * NI + ic
                        pe.wait_ge(*sum_made[i * GC * NI + n - 2])
                        pe.matmul(ps[:, n % 2, :], factors[g][:, ic * P:(ic + 1) * P], factors[g][:, D:2 * D],
                                  start=True, stop=True).then_inc(eff_made.sem, 1)
                pe.wait_ge(*o_loaded[i])
                for t in range(CT):
                    turn(i, t, o_in)
                pe.wait_ge(*w_cut[0])
                for t in range(CT):
                    pe.wait_ge(*t_cut[i * 2 * CT + t])
                    pe.wait_ge(*ffn_taken[i * CT + t - CT])
                    project(pe, ps[:, 4 + t, :], lambda h, ic: x_t[0][h][:, ic, t * P:(t + 1) * P],
                            lambda h, ic: w_out[h][:, ic, :], proj_made.sem)
                    if t >= 2:
                        pe.wait_ge(*norm_ok[i * CT + t - 2])
                        turn(i, CT + t - 2, x_n)
                ffn(i, 0)
                pe.wait_ge(*norm_ok[i * CT + 2])
                turn(i, CT + 2, x_n)
                ffn(i, 1)
                pe.wait_ge(*norm_ok[i * CT + 3])
                turn(i, CT + 3, x_n)
                ffn(i, 2)
                ffn(i, 3)


def kernel(L0_attn_x, L0_attn_Wq, L0_attn_bq, L0_attn_Wk, L0_attn_bk, L0_attn_Wv, L0_attn_bv, L0_attn_Wo,
           L0_attn_bo, L0_ffn_gate, L0_ffn_kernel, L0_ffn_bias, L0_ffn_lora_A, L0_ffn_lora_B,
           L0_ffn_lora_A_shared, L0_ffn_lora_B_shared):
    import numpy as np
    import concourse.bacc as bacc
    from concourse.bass_utils import run_bass_kernel_spmd

    def rows(v):
        return np.broadcast_to(np.asarray(v)[None, :], (P, D))

    shape = np.asarray(L0_attn_x).shape
    arrays = {
        "x": np.asarray(L0_attn_x).reshape(TOK, D),
        "wqT": np.asarray(L0_attn_Wq).T,
        "wkT": np.asarray(L0_attn_Wk).T,
        "wvT": np.asarray(L0_attn_Wv).T,
        "woT": np.asarray(L0_attn_Wo).T,
        "bq": np.asarray(L0_attn_bq).reshape(NI, P).T,
        "bk": np.asarray(L0_attn_bk).reshape(NI, P).T,
        "bv": rows(L0_attn_bv),
        "bo": rows(L0_attn_bo),
        "gate": np.repeat(np.asarray(L0_ffn_gate).T, RANK, axis=0),
        "ffn_w": np.asarray(L0_ffn_kernel),
        "ffn_b": rows(L0_ffn_bias),
        "lora_a": np.asarray(L0_ffn_lora_A).reshape(LORAS * RANK, D),
        "lora_b": np.asarray(L0_ffn_lora_B).transpose(0, 2, 1).reshape(LORAS * RANK, D),
        "lora_as": np.asarray(L0_ffn_lora_A_shared),
        "lora_bs": np.asarray(L0_ffn_lora_B_shared).T,
    }
    arrays = {n: np.ascontiguousarray(a) for n, a in arrays.items()}
    nc = bacc.Bacc("TRN2", target_bir_lowering=False, num_devices=1)
    args = [nc.dram_tensor(n, a.shape, mybir.dt.from_np(a.dtype), kind="ExternalInput").ap()
            for n, a in arrays.items()]
    out = nc.dram_tensor("out", (TOK, D), F32, kind="ExternalOutput").ap()
    build(nc, *args, out)
    r = run_bass_kernel_spmd(nc, [arrays], core_ids=[0])
    return r.results[0]["out"].reshape(shape)
```

```python
from contextlib import ExitStack

import concourse.bass as bass
from concourse import mybir

F32 = mybir.dt.float32
F32R = mybir.dt.float32r
BF16 = mybir.dt.bfloat16
ALU = mybir.AluOpType
ACT = mybir.ActivationFunctionType
AX = mybir.AxisListType

P = 128
D = 512
NI = D // P
HD = 16
HEADS = D // HD
TOK = 2048
SEQ = 1024
BATCH = TOK // SEQ
CH = 512
CT = CH // P
NCH = TOK // CH
GROUPS = 8
GT = TOK // GROUPS // P
GC = GROUPS // NCH
LORAS = 16
RANK = 32
LCH = LORAS * RANK // P
EPS = 1e-5
FMIN = -3.0e38

HG = 4
NG = HEADS // HG
UNITS = BATCH * NG
VC = HD + 1
PARTS = 3
TERMS = [(0, 0), (0, 1), (0, 2), (1, 0), (1, 1), (2, 0)]
KROWS = HD * len(TERMS)
SROWS = KROWS + 2
NPACK = 3
LOADS = 3 * len(TERMS) + 1
QT = SEQ // P
STEPS = [(c, kt) for c in range(2) for kt in range(CT * (c + 1))]
NS = len(STEPS)
DIAG = [s for s, (c, kt) in enumerate(STEPS) if kt >= CT * c]
PBUF = 3


class Events:

    def __init__(self, sem, step=1, ahead=0):
        self.sem, self.step, self.ahead = sem, step, ahead

    def __getitem__(self, n):
        return self.sem, (n + (self.ahead + 1)) * self.step


def give_ahead(eng, events):
    for e in events:
        if e.ahead:
            eng.sem_inc(e.sem, e.ahead * e.step)


def project(pe, psum, left, right, done=None):
    terms = [(0, 1), (1, 0), (0, 0)]
    for n, (a, b) in enumerate(terms):
        for ic in range(NI):
            last = pe.matmul(psum, left(a, ic), right(b, ic), start=(n == 0 and ic == 0),
                             stop=(done is not None and n == len(terms) - 1 and ic == NI - 1))
    if done is not None:
        last.then_inc(done, 1)


def low_rank_down(pe, psum, a_fac, x_t, g, done):
    terms = [(0, 1), (1, 0), (0, 0)]
    for n, (a, b) in enumerate(terms):
        for ic in range(NI):
            last = pe.matmul(psum, a_fac[a][:, g, ic, :, :, :].rearrange("p n s r -> p (n s r)"), x_t[b][:, ic, g * GT * P:(g + 1) * GT * P],
                             start=(n == 0 and ic == 0), stop=(n == len(terms) - 1 and ic == NI - 1))
    last.then_inc(done, 1)


def group_a_hi(act, a_fac, a_all, g, group, done):
    src = a_all[:, :, bass.ds(group, 1), :].to_broadcast([P, NI, 2, RANK])
    act.activation(a_fac[0][:, g, :, :, 0, :], src, ACT.Copy).then_inc(done, 1)


def group_a_lo(dve, a_fac, a_all, g, group, done):
    src = a_all[:, :, bass.ds(group, 1), :].to_broadcast([P, NI, 2, RANK])
    dve.tensor_tensor(a_fac[1][:, g, :, :, 0, :], src, a_fac[0][:, g, :, :, 0, :].bitcast(F32), ALU.subtract).then_inc(done, 1)


def low_rank_up(pe, psum, h_t, b_fac, group, done):
    for h in (1, 0):
        last = pe.matmul(psum, h_t, b_fac[h][:, bass.ds(group, 1), :].rearrange("p a d -> p (a d)"),
                         start=False, stop=(h == 0))
    last.then_inc(done, 1)


def build(nc, x, wqT, wkT, wvT, woT, bq, bk, bv, bo, gate, ffn_w, ffn_b, lora_a, lora_b, lora_as, lora_bs, out):
    with ExitStack() as whole:
        def dram(name, shape, dt):
            return nc.dram_tensor(name, shape, dt, kind="Internal").ap()

        def sb(name, shape, dt=F32):
            return whole.enter_context(nc.sbuf_tensor(name, shape, dt))

        b_scr = dram("b_scr", (GROUPS * RANK, D), F32)
        x1_scr = dram("x1_scr", (TOK, D), F32)
        q_scr = dram("q_scr", (PARTS, BATCH * D, SEQ), BF16)
        k_scr = dram("k_scr", (PARTS, BATCH * D, SEQ), BF16)
        v_scr = dram("v_scr", (UNITS, SEQ, HG * VC), F32)
        o_scr = dram("o_scr", (UNITS, SEQ, HG * HD), F32)

        with ExitStack() as raw:
            w_ffn_raw = raw.enter_context(nc.sbuf_tensor("w_ffn_raw", [P, NI, D], F32))
            b_raw = raw.enter_context(nc.sbuf_tensor("b_raw", [P, GROUPS, D], F32))
        w_ffn_lo = sb("w_ffn_lo", [P, NI, D], F32R)
        b_lo = sb("b_lo", [P, GROUPS, D], F32R)
        w_ffn, b_fac = [sb("w_ffn_hi", [P, NI, D], F32R), w_ffn_lo], [sb("b_hi", [P, GROUPS, D], F32R), b_lo]
        ident = sb("ident", [P, P])
        causal = sb("causal", [P, CH])
        ps = whole.enter_context(nc.psum_tensor("ps", [P, 8, 512], F32))
        small = sb("small", [P, 8])
        neg_half, eps = small[:, 0:1], small[:, 1:2]
        half_bias = sb("half_bias", [P, D])
        a_all = sb("a_all", [P, NI, GROUPS, RANK])
        a_fac = [sb(f"a_fac{h}", [P, GC, NI, 2, 2, RANK], F32R) for h in range(2)]
        shared = (ident, causal, ps, neg_half, eps, half_bias, w_ffn, a_all, a_fac, b_fac)

        stage_a(nc, shared, w_ffn_raw, b_raw, x, wqT, wkT, wvT, bq, bk, bv, bo, gate, ffn_w, ffn_b, lora_a, lora_b, lora_as, lora_bs,
                b_scr, x1_scr, q_scr, k_scr, v_scr)
        stage_b(nc, ps, ident, causal, q_scr, k_scr, v_scr, o_scr)
        stage_c(nc, shared, woT, x1_scr, o_scr, out)


def stage_a(nc, shared, w_ffn_raw, b_raw, x, wqT, wkT, wvT, bq, bk, bv, bo, gate, ffn_w, ffn_b, lora_a, lora_b, lora_as, lora_bs,
            b_scr, x1_scr, q_scr, k_scr, v_scr):
    ident, causal, ps, neg_half, eps, half_bias, w_ffn, a_all, a_fac, b_fac = shared
    with ExitStack() as ctx:
        every = []

        def sb(name, shape, dt=F32):
            return ctx.enter_context(nc.sbuf_tensor("a_" + name, shape, dt))

        def events(name, step=1, ahead=0):
            every.append(Events(ctx.enter_context(nc.semaphore("a_" + name)), step, ahead))
            return every[-1]

        with ExitStack() as raw:
            w_raw = [raw.enter_context(nc.sbuf_tensor(f"a_w_{n}_raw", [P, NI, D], F32)) for n in "qkv"]
            lora_ab = [raw.enter_context(nc.sbuf_tensor(f"adapters_{n}", [P, LCH, D], F32)) for n in "ab"]
        w_lo = [sb(f"w_{n}_lo", [P, NI, D], F32R) for n in "qkv"]
        w_qkv = [[sb(f"w_{n}_hi", [P, NI, D], F32R), w_lo["qkv".index(n)]] for n in "qkv"]
        x_in = sb("x_in", [P, CT, D])
        x_n = sb("x_n", [P, CT, D])
        x_t = [sb(f"x_t{h}", [P, NI, CH], F32R) for h in range(2)]
        x1 = sb("x1", [P, CT, D])
        h_t = sb("h_t", [P, GC, GT * P], F32R)
        x1_b = sb("x1_b", [P, 2, D])
        stats, moments = sb("stats", [P, 2, CT, 6]), sb("moments", [P, 2, CT, 2])
        var_eps, rstd = sb("var_eps", [P, 2, CT]), sb("rstd", [P, 2, CT])
        qk = sb("qk", [P, 2, CH])
        rest = sb("rest", [P, 2, CH])
        parts = sb("parts", [P, 2, PARTS, CH], BF16)
        v_tile = sb("v_tile", [P, 2, HEADS, VC])
        biases = sb("biases", [P, 2, D])
        b_qk = sb("b_qk", [P, 2, NI])
        gate_rows = sb("gate_rows", [P, LCH, GROUPS])
        delta = sb("delta", [P, RANK])
        spread = sb("spread", [P, LCH, GROUPS, RANK])
        as_in = sb("as_in", [P, NI, RANK])

        gate_in, adapters_in, as_loaded = events("gate_in", 16), [events("a_in", 16), events("b_in", 16)], events("as_in", 16)
        zeroed, spread_ok = events("zeroed"), events("spread_ok")
        down_made, down_taken, shared_hi, shared_cut = [events(s) for s in ("down_made", "down_taken", "shared_hi", "shared_cut")]
        a_hi, a_cut = events("a_hi"), events("a_cut")
        up_made, up_taken, up_out, b_loaded = events("up_made"), events("up_taken"), events("up_out", 16), events("b_loaded", 64)
        b_hi, b_cut = events("b_hi"), events("b_cut")
        wf_loaded, wf_hi, wf_cut = events("wf_loaded", 16), events("wf_hi"), events("wf_cut")
        w_loaded, w_hi, w_cut = [[events(f"w{n}_{s}", c) for n in range(3)] for s, c in (("loaded", 16), ("hi", 1), ("cut", 1))]
        params_in = events("params_in", 16 * 5)
        consts, scaled = events("consts"), events("scaled")
        x_loaded, xb_made = [events(f"x_loaded{t}", 16) for t in range(CT)], events("xb_made")
        st_ok, mom_ok, var_ok, rstd_ok, norm_ok = [[events(f"{s}{n}") for n in range(2)] for s in
                                                   ("st_ok", "mom_ok", "var_ok", "rstd_ok", "norm_ok")]
        turned, t_hi, t_cut = events("turned"), events("t_hi"), events("t_cut", ahead=2)
        h_made, h_hi, h_cut = events("h_made"), events("h_hi"), events("h_cut")
        ffn_made, ffn_taken = events("ffn_made", ahead=1), events("ffn_taken")
        v_made, v_taken = events("v_made"), events("v_taken")
        v_out = [events(f"v_out{n}", 16, 1) for n in range(2)]
        qk_made, qk_taken = events("qk_made", ahead=1), events("qk_taken", ahead=CT)
        part1, rest_ok, part2, qk_cut = events("part1"), events("rest_ok"), events("part2"), events("qk_cut", ahead=2)
        parts_out = [events(f"parts_out{n}", 16, 1) for n in range(2)]
        x1b_made, x1_out = events("x1b_made", ahead=CT), [events(f"x1_out{n}", 16, 1) for n in range(2)]

        waited = events("waited")

        block = ctx.enter_context(nc.Block())
        x_view = x.rearrange("(t p) d -> p t d", p=P)
        x1_view = x1_scr.rearrange("(t p) d -> p t d", p=P)

        @block.sync
        def _(sp):
            def load_x(tile, t):
                sp.dma_start(x_in[:, t:t + 1, :], x_view[:, bass.ds(tile, 1), :]).then_inc(x_loaded[t].sem, 16)

            def load_rows(dst, src, signal):
                sp.dma_start(dst, src.rearrange("(c p) d -> p c d", p=P)).then_inc(signal.sem, 16)

            sp.dma_start(gate_rows[:, :, :], gate.rearrange("(c p) b -> p c b", p=P)).then_inc(gate_in.sem, 16)
            load_x(0, 0)
            load_rows(lora_ab[0][:, :, :], lora_a, adapters_in[0])
            for t in range(1, CT):
                load_x(t, t)
            sp.dma_start(as_in[:, :, :], lora_as.rearrange("(c p) r -> p c r", p=P)).then_inc(as_loaded.sem, 16)
            load_rows(w_ffn_raw[:, :, :], ffn_w, wf_loaded)
            load_rows(lora_ab[1][:, :, :], lora_b, adapters_in[1])
            for dst, src in ((half_bias[:, :], ffn_b), (biases[:, 0, :], bv), (biases[:, 1, :], bo),
                             (b_qk[:, 0, :], bq), (b_qk[:, 1, :], bk)):
                sp.dma_start(dst, src).then_inc(params_in.sem, 16)
            load_rows(w_raw[2][:, :, :], wvT, w_loaded[2])
            for half in range(2):
                sp.wait_ge(*up_taken[half])
                sp.dma_start(b_scr[half * P:(half + 1) * P, :], x1[:, half, :]).then_inc(up_out.sem, 16)
            sp.wait_ge(*up_out[1])
            for at in (0, 2 * RANK):
                sp.dma_start(b_raw[at:at + RANK, :, :],
                             b_scr.rearrange("(b r) d -> r b d", r=RANK)).then_inc(b_loaded.sem, 16)
                sp.dma_start(b_raw[at + RANK:at + 2 * RANK, :, :],
                             lora_bs.unsqueeze(1).to_broadcast([RANK, GROUPS, D])).then_inc(b_loaded.sem, 16)
            load_rows(w_raw[0][:, :, :], wqT, w_loaded[0])
            load_rows(w_raw[1][:, :, :], wkT, w_loaded[1])

            def chunk(i, last):
                row, half = i // 2, i % 2
                for t in range(CT):
                    if not last:
                        sp.wait_ge(*ffn_taken[i * CT + t])
                        load_x((i + 1) * CT + t, t)
                    sp.wait_ge(*x1b_made[i * CT + t])
                    sp.dma_start(x1_view[:, bass.ds(i * CT + t, 1), :],
                                 x1_b[:, t % 2:t % 2 + 1, :]).then_inc(x1_out[t % 2].sem, 16)
                for t in range(CT):
                    sp.wait_ge(*v_taken[i * CT + t])
                    dst = v_scr[bass.ds(row * NG, NG), bass.ds(half * CH + t * P, P), :].rearrange("g p v -> p g v")
                    src = v_tile[:, t % 2, :, :].rearrange("p (g h) v -> p g (h v)", g=NG)
                    sp.dma_start(dst, src).then_inc(v_out[t % 2].sem, 16)
                for j in range(2 * NI):
                    scr = (q_scr, k_scr)[j // NI]
                    sp.wait_ge(*qk_cut[i * 2 * NI + j])
                    dst = scr[:, bass.ds(row * D + (j % NI) * P, P), bass.ds(half * CH, CH)].rearrange("s p n -> p s n")
                    sp.dma_start(dst, parts[:, j % 2, :, :]).then_inc(parts_out[j % 2].sem, 16)

            with sp.Fori(0, NCH - 1) as i:
                chunk(i, False)
            chunk(NCH - 1, True)
            for n in range(2):
                sp.wait_ge(*x1_out[n][NCH * CT // 2 - 1])
                sp.wait_ge(*v_out[n][NCH * CT // 2 - 1])
                sp.wait_ge(*parts_out[n][NCH * NI - 1])

        @block.gpsimd
        def _(pool):
            give_ahead(pool, every)
            pool.memset(delta[:, :], 0.0).then_inc(zeroed.sem, 1)
            for n in range(P // RANK):
                pool.wait_ge(*zeroed[n])
                pool.affine_select(out=delta[:, :], in_=delta[:, :], compare_op=ALU.not_equal, fill=1.0,
                                   base=-n * RANK, pattern=[[-1, RANK]], channel_multiplier=1).then_inc(zeroed.sem, 1)
            pool.memset(neg_half, -0.5).then_inc(consts.sem, 1)
            pool.memset(eps, EPS).then_inc(consts.sem, 1)
            pool.memset(ident[:, :], 0.0).then_inc(consts.sem, 1)
            pool.memset(causal[:, :], 0.0).then_inc(consts.sem, 1)
            pool.wait_ge(*consts[3])
            pool.affine_select(out=ident[:, :], in_=ident[:, :], compare_op=ALU.not_equal, fill=1.0, base=0,
                               pattern=[[-1, P]], channel_multiplier=1).then_inc(consts.sem, 1)
            pool.affine_select(out=causal[:, CH - P:CH], in_=causal[:, CH - P:CH], compare_op=ALU.is_ge,
                               fill=FMIN, base=0, pattern=[[-1, P]], channel_multiplier=1).then_inc(consts.sem, 1)
            pool.memset(v_tile[:, :, :, HD:VC], 1.0).then_inc(consts.sem, 1)

            def rstd_of(ln, i, t):
                pool.wait_ge(*mom_ok[ln][i * CT + t])
                pool.tensor_tensor(var_eps[:, ln, t:t + 1], moments[:, ln, t, 1:2], eps, ALU.add).then_inc(var_ok[ln].sem, 1)
                pool.wait_ge(*var_ok[ln][i * CT + t])
                pool.tensor_tensor(rstd[:, ln, t:t + 1], var_eps[:, ln, t:t + 1], neg_half,
                                   ALU.pow).then_inc(rstd_ok[ln].sem, 1)

            def add_bias(i, t):
                pool.wait_ge(*norm_ok[0][i * CT + t])
                pool.tensor_tensor(x_in[:, t, :], x_in[:, t, :], half_bias[:, :], ALU.add).then_inc(xb_made.sem, 1)

            def store_x1(i, t):
                pool.wait_ge(*ffn_taken[i * CT + t])
                pool.wait_ge(*x1_out[t % 2][i * (CT // 2) + t // 2 - 1])
                pool.tensor_tensor(x1_b[:, t % 2, :], x1[:, t, :], biases[:, 1, :], ALU.add).then_inc(x1b_made.sem, 1)

            def chunk(i, last):
                for t in range(CT):
                    rstd_of(1, i, t)
                    if t:
                        store_x1(i, t - 1)
                store_x1(i, CT - 1)
                if not last:
                    for t in range(CT):
                        rstd_of(0, i + 1, t)
                    for t in range(CT):
                        add_bias(i + 1, t)

            for t in range(CT):
                rstd_of(0, 0, t)
            pool.wait_ge(*params_in[0])
            pool.tensor_scalar(half_bias[:, :], half_bias[:, :], 0.5, None, ALU.mult).then_inc(scaled.sem, 1)
            pool.tensor_scalar(b_qk[:, 0, :], b_qk[:, 0, :], float(HD) ** -0.5, None, ALU.mult).then_inc(scaled.sem, 1)
            pool.wait_ge(*scaled[0])
            for t in range(CT):
                add_bias(0, t)
            with pool.Fori(0, NCH - 1) as i:
                chunk(i, False)
            chunk(NCH - 1, True)

        @block.scalar
        def _(act):
            def turn_hi(i, n):
                act.wait_ge(*turned[i * 2 * CT + n])
                if n >= CT:
                    act.wait_ge(*ffn_made[i * CT + n - CT])
                at = n % CT * P
                act.activation(x_t[0][:, :, at:at + P], ps[:, 2 + n % 2, :].rearrange("p (c n) -> p c n", c=NI),
                               ACT.Copy).then_inc(t_hi.sem, 1)

            def second_part(i, j):
                act.wait_ge(*rest_ok[i * 2 * NI + j])
                act.activation(parts[:, j % 2, 1, :], rest[:, j % 2, :], ACT.Copy).then_inc(part2.sem, 1)

            def weights(n):
                act.wait_ge(*w_loaded[n][0])
                if n < 2:
                    for half in range(2):
                        act.wait_ge(*up_made[half])
                act.activation(w_qkv[n][0][:, :, :], w_raw[n][:, :, :], ACT.Copy).then_inc(w_hi[n].sem, 1)

            def chunk(i, first):
                act.wait_ge(*qk_made[i * 2 * NI - 1])
                for n in range(CT):
                    turn_hi(i, n)
                for g in range(GC):
                    group_a_hi(act, a_fac, a_all, g, i * GC + g, a_hi.sem)
                for g in range(GC):
                    act.wait_ge(*h_made[i * GC + g])
                    act.wait_ge(*ffn_made[i * CT - 1])
                    act.activation(h_t[:, g, :], ps[:, g, 0:GT * P], ACT.Copy).then_inc(h_hi.sem, 1)
                if first:
                    act.wait_ge(*b_loaded[0])
                for g in range(GC):
                    group = bass.ds(i * GC + g, 1)
                    act.activation(b_fac[0][:, group, :], b_raw[:, group, :], ACT.Copy).then_inc(b_hi.sem, 1)
                if first:
                    weights(2)
                turn_hi(i, CT)
                turn_hi(i, CT + 1)
                if first:
                    weights(0)
                turn_hi(i, CT + 2)
                turn_hi(i, CT + 3)
                if first:
                    weights(1)
                    act.wait_ge(*scaled[1])
                for j in range(2 * NI):
                    kq, n = j // NI, i * 2 * NI + j
                    act.wait_ge(*qk_made[n])
                    act.wait_ge(*qk_cut[n - 2])
                    act.activation(qk[:, j % 2, :], ps[:, 4 + j % 4, :], ACT.Identity,
                                   bias=b_qk[:, kq, j % NI:j % NI + 1],
                                   scale=(float(HD) ** -0.5, 1.0)[kq]).then_inc(qk_taken.sem, 1)
                    act.wait_ge(*qk_taken[n])
                    act.wait_ge(*parts_out[j % 2][i * NI + j // 2 - 1])
                    act.activation(parts[:, j % 2, 0, :], qk[:, j % 2, :], ACT.Copy).then_inc(part1.sem, 1)
                    if j:
                        second_part(i, j - 1)
                second_part(i, 2 * NI - 1)

            act.wait_ge(*as_loaded[0])
            for g in range(GC):
                act.activation(a_fac[0][:, g, :, :, 1, :], as_in[:, :, :].unsqueeze(2).to_broadcast([P, NI, 2, RANK]),
                               ACT.Copy).then_inc(shared_hi.sem, 1)
            for ic in range(NI):
                act.wait_ge(*down_made[ic])
                act.activation(a_all[:, ic, :, :], ps[:, ic, 0:GROUPS * RANK].rearrange("p (b r) -> p b r", b=GROUPS),
                               ACT.Copy).then_inc(down_taken.sem, 1)
            act.wait_ge(*down_taken[NI - 1])
            act.wait_ge(*wf_loaded[0])
            for ic in range(NI):
                act.activation(w_ffn[0][:, ic, :], w_ffn_raw[:, ic, :], ACT.Copy).then_inc(wf_hi.sem, 1)
            chunk(0, True)
            with act.Fori(1, NCH) as i:
                chunk(i, False)

        @block.vector
        def _(dve):
            def norm(ln, i, t, rows):
                dve.bn_stats(stats[:, ln, t, :], rows).then_inc(st_ok[ln].sem, 1)
                dve.wait_ge(*st_ok[ln][i * CT + t])
                dve.sem_inc(waited.sem, 1)
                dve.bn_aggr(moments[:, ln, t, :], stats[:, ln, t, :]).then_inc(mom_ok[ln].sem, 1)

            def norm_out(ln, i, t, rows):
                dve.wait_ge(*rstd_ok[ln][i * CT + t])
                dve.tensor_scalar(x_n[:, t, :], rows, moments[:, ln, t, 0:1], rstd[:, ln, t:t + 1],
                                  ALU.subtract, ALU.mult).then_inc(norm_ok[ln].sem, 1)

            def turn_lo(i, n):
                dve.wait_ge(*t_hi[i * 2 * CT + n])
                at = n % CT * P
                dve.tensor_tensor(x_t[1][:, :, at:at + P], ps[:, 2 + n % 2, :].rearrange("p (c n) -> p c n", c=NI),
                                  x_t[0][:, :, at:at + P].bitcast(F32), ALU.subtract).then_inc(t_cut.sem, 1)

            def lo_part(pair, raw, *at):
                return dve.tensor_tensor(pair[1][at], raw[at], pair[0][at].bitcast(F32), ALU.subtract)

            def weights(n):
                dve.wait_ge(*w_hi[n][0])
                lo_part(w_qkv[n], w_raw[n], slice(None), slice(None), slice(None)).then_inc(w_cut[n].sem, 1)

            def third_part(i, j):
                dve.wait_ge(*part2[i * 2 * NI + j])
                dve.tensor_tensor(parts[:, j % 2, 2, :], rest[:, j % 2, :], parts[:, j % 2, 1, :],
                                  ALU.subtract).then_inc(qk_cut.sem, 1)

            def ffn_sum(i, t):
                dve.wait_ge(*ffn_made[i * CT + t])
                dve.wait_ge(*xb_made[i * CT + t])
                dve.wait_ge(*x1b_made[i * CT + t - CT])
                dve.scalar_tensor_tensor(out=x1[:, t, :], in0=ps[:, 4 + t, :], scalar=0.5, in1=x_in[:, t, :],
                                         op0=ALU.mult, op1=ALU.add).then_inc(ffn_taken.sem, 1)
                dve.wait_ge(*ffn_taken[i * CT + t])
                norm(1, i, t, x1[:, t, :])

            def v_sum(i, t):
                dve.wait_ge(*v_made[i * CT + t])
                dve.wait_ge(*v_out[t % 2][i * (CT // 2) + t // 2 - 1])
                dve.tensor_tensor(v_tile[:, t % 2, :, 0:HD], ps[:, 4 + t, :].rearrange("p (h d) -> p h d", h=HEADS),
                                  biases[:, 0, :].rearrange("p (h d) -> p h d", h=HEADS), ALU.add).then_inc(v_taken.sem, 1)

            def chunk(i, first, last):
                for t in range(CT):
                    turn_lo(i, t)
                for g in range(GC):
                    dve.wait_ge(*a_hi[i * GC + g])
                    group_a_lo(dve, a_fac, a_all, g, i * GC + g, a_cut.sem)
                for g in range(GC):
                    dve.wait_ge(*h_hi[i * GC + g])
                    dve.tensor_tensor(h_t[P // 2:P, g, :], ps[P // 2:P, g, 0:GT * P], h_t[P // 2:P, g, :].bitcast(F32),
                                      ALU.subtract).then_inc(h_cut.sem, 1)
                for g in range(GC):
                    dve.wait_ge(*b_hi[i * GC + g])
                    lo_part(b_fac, b_raw, slice(None), bass.ds(i * GC + g, 1), slice(None)).then_inc(b_cut.sem, 1)
                if first:
                    weights(2)
                ffn_sum(i, 0)
                ffn_sum(i, 1)
                norm_out(1, i, 0, x1[:, 0, :])
                norm_out(1, i, 1, x1[:, 1, :])
                ffn_sum(i, 2)
                turn_lo(i, CT)
                norm_out(1, i, 2, x1[:, 2, :])
                ffn_sum(i, 3)
                turn_lo(i, CT + 1)
                norm_out(1, i, 3, x1[:, 3, :])
                if first:
                    weights(0)
                v_sum(i, 0)
                turn_lo(i, CT + 2)
                v_sum(i, 1)
                turn_lo(i, CT + 3)
                if first:
                    weights(1)
                v_sum(i, 2)
                v_sum(i, 3)
                for j in range(2 * NI):
                    dve.wait_ge(*part1[i * 2 * NI + j])
                    dve.tensor_tensor(rest[:, j % 2, :], qk[:, j % 2, :], parts[:, j % 2, 0, :],
                                      ALU.subtract).then_inc(rest_ok.sem, 1)
                    if j:
                        third_part(i, j - 1)
                    if not last and j < CT:
                        dve.wait_ge(*x_loaded[j][i + 1])
                        norm(0, i + 1, j, x_in[:, j, :])
                    if not last and 2 <= j < CT + 2:
                        norm_out(0, i + 1, j - 2, x_in[:, j - 2, :])
                third_part(i, 2 * NI - 1)

            dve.wait_ge(*zeroed[P // RANK])
            dve.wait_ge(*gate_in[0])
            for c in range(LCH):
                dve.tensor_tensor(spread[:, c, :, :],
                                  delta[:, :].unsqueeze(1).to_broadcast([P, GROUPS, RANK]),
                                  gate_rows[:, c, :].unsqueeze(2).to_broadcast([P, GROUPS, RANK]),
                                  ALU.mult).then_inc(spread_ok.sem, 1)
            for t in range(CT):
                dve.wait_ge(*x_loaded[t][0])
                norm(0, 0, t, x_in[:, t, :])
            for t in range(CT):
                norm_out(0, 0, t, x_in[:, t, :])
            for g in range(GC):
                dve.wait_ge(*shared_hi[g])
                dve.tensor_tensor(a_fac[1][:, g, :, :, 1, :], as_in[:, :, :].unsqueeze(2).to_broadcast([P, NI, 2, RANK]),
                                  a_fac[0][:, g, :, :, 1, :].bitcast(F32), ALU.subtract).then_inc(shared_cut.sem, 1)
            for ic in range(NI):
                dve.wait_ge(*wf_hi[ic])
                lo_part(w_ffn, w_ffn_raw, slice(None), ic, slice(None)).then_inc(wf_cut.sem, 1)
            for half in range(2):
                dve.wait_ge(*up_made[half])
                dve.tensor_copy(x1[:, half, :], ps[:, 4 + half, :]).then_inc(up_taken.sem, 1)
            dve.wait_ge(*consts[6])
            dve.wait_ge(*params_in[0])
            dve.wait_ge(*up_out[1])
            chunk(0, True, False)
            with dve.Fori(1, NCH - 1) as i:
                chunk(i, False, False)
            chunk(NCH - 1, False, True)

        @block.tensor
        def _(pe):
            def turn(i, n):
                ln, t = n // CT, n % CT
                pe.wait_ge(*norm_ok[ln][i * CT + t])
                pe.wait_ge(*t_cut[i * 2 * CT + n - 2])
                for ic in range(NI):
                    mm = pe.transpose(ps[:, 2 + n % 2, ic * P:(ic + 1) * P], x_n[:, t, ic * P:(ic + 1) * P], ident[:, :])
                mm.then_inc(turned.sem, 1)

            def rows(t):
                return lambda h, ic: x_t[h][:, ic, t * P:(t + 1) * P]

            def ffn_base(i, t):
                pe.wait_ge(*t_cut[i * 2 * CT + t])
                pe.wait_ge(*qk_taken[i * 2 * NI - CT + t])
                project(pe, ps[:, 4 + t, :], rows(t), lambda h, ic: w_ffn[h][:, ic, :])

            def down(i, g):
                pe.wait_ge(*t_cut[i * 2 * CT + (g + 1) * GT - 1])
                pe.wait_ge(*a_cut[i * GC + g])
                low_rank_down(pe, ps[:, g, 0:GT * P], a_fac, x_t, g, h_made.sem)

            def up(i, t):
                g = t // GT
                pe.wait_ge(*h_cut[i * GC + g])
                pe.wait_ge(*b_cut[i * GC + g])
                low_rank_up(pe, ps[:, 4 + t, :], h_t[:, g, t % GT * P:(t % GT + 1) * P], b_fac, i * GC + g, ffn_made.sem)

            def v_rows(i, t):
                pe.wait_ge(*t_cut[i * 2 * CT + CT + t])
                pe.wait_ge(*ffn_taken[i * CT + t])
                pe.wait_ge(*w_cut[2][0])
                project(pe, ps[:, 4 + t, :], rows(t), lambda h, ic: w_qkv[2][h][:, ic, :], v_made.sem)

            pe.wait_ge(*spread_ok[LCH - 1])
            pe.wait_ge(*adapters_in[0][0])
            for ic in range(NI):
                for c in range(LCH):
                    mm = pe.matmul(ps[:, ic, 0:GROUPS * RANK], lora_ab[0][:, c, ic * P:(ic + 1) * P],
                                   spread[:, c, :, :].rearrange("p b r -> p (b r)"), start=(c == 0), stop=(c == LCH - 1))
                mm.then_inc(down_made.sem, 1)
            pe.wait_ge(*adapters_in[1][0])
            for half in range(2):
                for c in range(LCH):
                    g = spread[:, c, half * GROUPS // 2:(half + 1) * GROUPS // 2, :].rearrange("p b r -> p (b r)")
                    mm = pe.matmul(ps[:, 4 + half, :], g, lora_ab[1][:, c, :], start=(c == 0), stop=(c == LCH - 1))
                mm.then_inc(up_made.sem, 1)
            pe.wait_ge(*consts[4])
            pe.wait_ge(*shared_cut[GC - 1])
            pe.wait_ge(*down_taken[NI - 1])
            pe.wait_ge(*wf_cut[NI - 1])
            for half in range(2):
                pe.wait_ge(*up_taken[half])

            def chunk(i):
                turn(i, 0)
                turn(i, 1)
                ffn_base(i, 0)
                turn(i, 2)
                turn(i, 3)
                ffn_base(i, 1)
                down(i, 0)
                down(i, 1)
                ffn_base(i, 2)
                up(i, 0)
                up(i, 1)
                ffn_base(i, 3)
                up(i, 2)
                up(i, 3)
                turn(i, CT)
                turn(i, CT + 1)
                v_rows(i, 0)
                turn(i, CT + 2)
                v_rows(i, 1)
                turn(i, CT + 3)
                v_rows(i, 2)
                v_rows(i, 3)
                for j in range(2 * NI):
                    at = j % NI * P
                    if j < CT:
                        pe.wait_ge(*v_taken[i * CT + j])
                    else:
                        pe.wait_ge(*qk_taken[i * 2 * NI + j - CT])
                    pe.wait_ge(*w_cut[j // NI][0])
                    project(pe, ps[:, 4 + j % 4, :], lambda h, ic: w_qkv[j // NI][h][:, ic, at:at + P],
                            lambda h, ic: x_t[h][:, ic, :], qk_made.sem)

            with pe.Fori(0, NCH) as i:
                chunk(i)


def score_jobs():
    first = [("max", 0, h, q, 0, (q + 1) * P) for q in range(CT) for h in range(HG)]
    second = []
    for q in range(CT):
        for h in range(HG):
            second += [("max", 1, h, q, 0, CH), ("max", 1, h, q, CH, (q + 1) * P)]
    return first, second


def stage_b(nc, ps, ident, causal, q_scr, k_scr, v_scr, o_scr):
    with ExitStack() as ctx:
        every = []

        def sb(name, shape, dt=F32):
            return ctx.enter_context(nc.sbuf_tensor("b_" + name, shape, dt))

        def events(name, step=1, ahead=0):
            every.append(Events(ctx.enter_context(nc.semaphore("b_" + name)), step, ahead))
            return every[-1]

        S_BANK, O_BANK, RING, NRING = 0, 4, 5, 3
        AHEAD = 2

        q_pack = [sb(f"q_pack{n}", [SROWS, 2, HG, CH], BF16) for n in range(NPACK)]
        k_pack = [sb(f"k_pack{n}", [SROWS, HG, SEQ], BF16) for n in range(NPACK)]
        v_pack = [sb(f"v_pack{n}", [P, QT, HG * VC]) for n in range(NPACK)]
        probs = sb("probs", [P, PBUF, HG, CH])
        top = sb("top", [P, 4, HG * CT])
        neg_top = sb("neg_top", [HG * CT, 2, 2, P], BF16)
        o_t = sb("o_t", [P, 2, CH])
        inv = sb("inv", [P, 2, HG * CT])
        o_rows = sb("o_rows", [P, 2, HG * CT, HD])

        def width(s):
            c, kt = STEPS[s]
            return CH - max(0, kt - CT * c) * P

        first, second = score_jobs()
        ring_start = first + [("turn", 0)] + second
        J0 = len(ring_start)

        def jobs_by_step():
            todo = first + [("turn", 0)] + second
            cost = [75 + (job[5] if job[0] == "max" else P) for job in todo]
            all_cost, all_width = sum(cost), sum(map(width, range(NS)))
            by_step, given = [], 0.0
            for s in range(NS):
                now = [("turn", 1)] if s == 0 else []
                goal = all_cost * sum(map(width, range(s + 1))) / all_width
                while todo and given + cost[0] / 2 <= goal:
                    now.append(todo.pop(0))
                    given += cost.pop(0)
                if s == CT + OUT_LAG:
                    now.append(("out", 0))
                by_step.append(now)
            return by_step[:-1] + [by_step[-1] + todo + [("out", 1)]]

        OUT_LAG = 0
        by_step = jobs_by_step()
        ring = sum(by_step, [])
        J = len(ring)
        tail = [[("turn", 1)] if s == 0 else [("out", 0)] if s == CT + OUT_LAG else [("out", 1)] if s == NS - 1 else []
                for s in range(NS)]

        EMPTY = (20, 36)
        slot = [n + sum(n >= e for e in EMPTY) for n in range(J)]
        SLOTS = J + len(EMPTY)
        SHIFT = -J0 % NRING
        assert SLOTS % NRING == 0

        def bank(n):
            return RING + slot[n] % NRING

        def earlier(n):
            s = slot[n]
            while True:
                s -= NRING
                if s < 0:
                    return slot.index(s + SLOTS) - J
                if s in slot:
                    return slot.index(s)

        def ring_of(more):
            return ring if more else sum(tail, [])

        loaded = [events(f"loaded{n}", 16 * LOADS) for n in range(NPACK)]
        ones_ok = events("ones_ok", NPACK * 2 + 1)
        ring_made, ring_taken = events("ring_made"), events("ring_taken", ahead=NRING)
        top_ok, neg_hi = events("top_ok"), events("neg_hi")
        neg_in = [events(f"neg_in{c}", 32, 1) for c in range(2)]
        s_made, s_taken = events("s_made"), events("s_taken", ahead=2)
        masked = events("masked")
        pv_made = events("pv_made", ahead=PBUF)
        o_taken = events("o_taken", ahead=1)
        inv_ok = events("inv_ok")
        o_out = [events(f"o_out{c}", 16, 1) for c in range(2)]

        waited = events("waited")

        block = ctx.enter_context(nc.Block())

        TRIPLES = (UNITS - 2) // NPACK

        def over_units(eng, unit):
            with eng.Fori(0, TRIPLES) as i:
                for r in range(NPACK):
                    unit(i * NPACK + r, r, i, True, True)
            for u in range(TRIPLES * NPACK, UNITS):
                unit(u, u % NPACK, u // NPACK, u + 1 < UNITS, u + 2 < UNITS)

        @block.sync
        def _(sp):
            def load(u, r):
                rows = HG * HD
                for n, (q_part, k_part) in enumerate(TERMS):
                    at = slice(n * HD, (n + 1) * HD)
                    for c in range(2):
                        src = q_scr[q_part, bass.ds(u * rows, rows), c * CH:(c + 1) * CH].rearrange("(h d) n -> d h n", h=HG)
                        sp.dma_start(q_pack[r][at, c, :, :], src).then_inc(loaded[r].sem, 16)
                    src = k_scr[k_part, bass.ds(u * rows, rows), :].rearrange("(h d) n -> d h n", h=HG)
                    sp.dma_start(k_pack[r][at, :, :], src).then_inc(loaded[r].sem, 16)
                src = v_scr[bass.ds(u, 1), :, :].rearrange("a (t p) v -> p (a t) v", p=P)
                sp.dma_start(v_pack[r][:, :, :], src).then_inc(loaded[r].sem, 16)

            def neg_rows(u, r, c, taken):
                sp.wait_ge(*taken)
                for part in range(2):
                    sp.dma_start(q_pack[r][KROWS + part:KROWS + part + 1, c, :, :].rearrange("a h n -> a (h n)"),
                                 neg_top[:, c, part, :]).then_inc(neg_in[c].sem, 16)

            def store(u, c, taken):
                sp.wait_ge(*taken)
                dst = o_scr[bass.ds(u, 1), c * CH:(c + 1) * CH, :].rearrange("a (t p) v -> p (a t) v", p=P)
                sp.dma_start(dst, o_rows[:, c, :, :].rearrange("p (t h) d -> p t (h d)", t=CT)).then_inc(o_out[c].sem, 16)

            def unit(u, r, i, more, more2):
                neg_rows(u, r, 1, ring_taken[u * J + (J0 + ring.index(("turn", 1)))])
                if more2:
                    sp.wait_ge(*pv_made[u * NS - 1])
                    load(u + 2, (r + 2) % NPACK)
                outs = [n for n, job in enumerate(ring_of(more)) if job[0] == "out"]
                store(u, 0, ring_taken[u * J + (J0 + outs[0])])
                if more:
                    neg_rows(u + 1, (r + 1) % NPACK, 0, ring_taken[u * J + (J0 + ring.index(("turn", 0)))])
                store(u, 1, ring_taken[u * J + (J0 + outs[1])])

            load(0, 0)
            load(1, 1)
            neg_rows(0, 0, 0, ring_taken[len(first)])
            over_units(sp, unit)
            for c in range(2):
                sp.wait_ge(*o_out[c][UNITS - 1])

        @block.gpsimd
        def _(pool):
            give_ahead(pool, every)
            for n in range(NPACK):
                pool.memset(k_pack[n][KROWS:SROWS, :, :], 1.0).then_inc(ones_ok.sem, 1)

            def unit(u, r, i, more, more2):
                for s in DIAG:
                    pool.wait_ge(*s_taken[u * 2 * NS + 2 * s + 1])
                    pool.sem_inc(waited.sem, 1)
                    block_ = probs[:, s % PBUF, :, 0:P]
                    pool.affine_select(out=block_, in_=block_, compare_op=ALU.is_ge, fill=0.0, base=0,
                                       pattern=[[0, HG], [1, P]], channel_multiplier=-1).then_inc(masked.sem, 1)

            with pool.Fori(0, UNITS) as u:
                unit(u, None, None, None, None)

        @block.scalar
        def _(act):
            def exps(u, s):
                c, kt = STEPS[s]
                width = CH - max(0, kt - CT * c) * P
                act.wait_ge(*pv_made[u * NS + s - PBUF])
                for half in range(2):
                    act.wait_ge(*s_made[u * 2 * NS + 2 * s + half])
                    act.activation(probs[:, s % PBUF, 2 * half:2 * half + 2, 0:width],
                                   ps[:, S_BANK + 2 * half:S_BANK + 2 * half + 2, 0:width], ACT.Exp).then_inc(s_taken.sem, 1)

            def take_out(u, c):
                last = [n for n, (cc, _) in enumerate(STEPS) if cc == c][-1]
                act.wait_ge(*pv_made[u * NS + last])
                act.activation(o_t[:, c, :], ps[:, O_BANK, :], ACT.Copy).then_inc(o_taken.sem, 1)

            def unit(u, more):
                for s in range(1, NS):
                    exps(u, s)
                    if s == CT:
                        take_out(u, 0)
                if more:
                    exps(u + 1, 0)
                take_out(u, 1)

            act.wait_ge(*ones_ok[0])
            exps(0, 0)
            with act.Fori(0, UNITS - 1) as u:
                unit(u, True)
            unit(UNITS - 1, False)

        @block.vector
        def _(dve):
            dve.memset(ps[:, O_BANK, :], 0.0).then_inc(ones_ok.sem, 1)
            for n in range(NPACK):
                dve.memset(q_pack[n][KROWS:SROWS, :, :, :], 0.0).then_inc(ones_ok.sem, 1)

            def job(what, n, n_bank, u):
                dve.wait_ge(*ring_made[n])
                if what[0] == "max":
                    _, c, h, q, a, w = what
                    at = h * CT + q
                    if a == 0 and w == CH and c == 1:
                        dve.tensor_reduce(top[:, 1, at:at + 1], ps[:, n_bank, :], AX.X, ALU.max).then_inc(ring_taken.sem, 1)
                    else:
                        dve.sem_inc(waited.sem, 1)
                        dve.tensor_tensor_reduce(ps[:, n_bank, 0:w], ps[:, n_bank, 0:w], causal[:, CH - w:CH], 1.0, FMIN,
                                                 ALU.add, ALU.max, top[:, 2 * c, at:at + 1]).then_inc(ring_taken.sem, 1)
                elif what[0] == "turn":
                    c = what[1]
                    dve.wait_ge(*neg_in[c][(u + (1 - c)) - 1])
                    dve.tensor_scalar(neg_top[:, c, 0, :], ps[0:HG * CT, n_bank, 0:P], -1.0, None,
                                      ALU.mult).then_inc(neg_hi.sem, 1)
                    dve.wait_ge(*neg_hi[u * 2 + (2 - c)])
                    dve.scalar_tensor_tensor(out=neg_top[:, c, 1, :], in0=ps[0:HG * CT, n_bank, 0:P], scalar=-1.0,
                                             in1=neg_top[:, c, 0, :], op0=ALU.mult,
                                             op1=ALU.subtract).then_inc(ring_taken.sem, 1)
                else:
                    c = what[1]
                    banks = ps[:, n_bank, :].rearrange("p (n v) -> p n v", v=32)
                    dve.reciprocal(inv[:, c, :].unsqueeze(2), banks[:, :, HD:VC]).then_inc(inv_ok.sem, 1)
                    dve.wait_ge(*inv_ok[u * 2 + c])
                    dve.wait_ge(*o_out[c][u - 1])
                    dve.tensor_tensor(o_rows[:, c, :, :], banks[:, :, 0:HD],
                                      inv[:, c, :].unsqueeze(2).to_broadcast([P, HG * CT, HD]),
                                      ALU.mult).then_inc(ring_taken.sem, 1)

            def join_top(u, n):
                dve.wait_ge(*ring_taken[n])
                dve.tensor_tensor(top[:, 3, :], top[:, 1, :], top[:, 2, :], ALU.max).then_inc(top_ok.sem, 1)

            for n, what in enumerate(ring_start):
                job(what, n, RING + (n + SHIFT) % NRING, -1)
            join_top(0, J0 - 1)

            def unit(u, r, i, more, more2):
                for n, what in enumerate(ring_of(more)):
                    job(what, u * J + (J0 + n), bank(n), u)
                    if what == second[-1]:
                        join_top(u + 1, u * J + (J0 + n))

            with dve.Fori(0, UNITS - 1) as u:
                unit(u, None, None, True, True)
            unit(UNITS - 1, None, None, False, False)

        @block.tensor
        def _(pe):
            def job(what, n, n_bank, free, r, u, half0):
                pe.wait_ge(*ring_taken[free])
                if what[0] == "max":
                    _, c, h, q, a, w = what
                    mm = pe.matmul(ps[:, n_bank, 0:w], q_pack[r][0:KROWS, c, h, q * P:(q + 1) * P], k_pack[r][0:KROWS, h, a:a + w],
                                   start=True, stop=True)
                elif what[0] == "turn":
                    c = what[1]
                    if c == 0:
                        pe.wait_ge(*ring_taken[half0])
                    else:
                        pe.wait_ge(*top_ok[u])
                    mm = pe.transpose(ps[0:HG * CT, n_bank, 0:P], top[:, 3 * c, :], ident[:, :])
                else:
                    c = what[1]
                    pe.wait_ge(*o_taken[u * 2 + c])
                    for q in range(CT):
                        mm = pe.transpose(ps[:, n_bank, q * P:(q + 1) * P], o_t[:, c, q * P:(q + 1) * P], ident[:, :])
                mm.then_inc(ring_made.sem, 1)

            def scores(u, r, s, half):
                c, kt = STEPS[s]
                skip = max(0, kt - CT * c) * P
                if half == 0 and (s == 0 or STEPS[s - 1][0] != c):
                    pe.wait_ge(*neg_in[c][u])
                pe.wait_ge(*s_taken[u * 2 * NS + 2 * s + half - 2])
                for h in range(2 * half, 2 * half + 2):
                    mm = pe.matmul(ps[:, S_BANK + h, 0:CH - skip], k_pack[r][:, h, kt * P:(kt + 1) * P],
                                   q_pack[r][:, c, h, skip:CH], start=True, stop=True)
                mm.then_inc(s_made.sem, 1)

            def values(u, r, s):
                c, kt = STEPS[s]
                skip = max(0, kt - CT * c) * P
                if s in DIAG:
                    pe.wait_ge(*masked[u * len(DIAG) + DIAG.index(s)])
                else:
                    pe.wait_ge(*s_taken[u * 2 * NS + 2 * s + 1])
                if kt == 0:
                    pe.wait_ge(*o_taken[u * 2 + c - 1])
                for h in range(HG):
                    mm = pe.matmul(ps[32 * h:32 * h + VC, O_BANK, skip:CH], v_pack[r][:, kt, h * VC:(h + 1) * VC],
                                   probs[:, s % PBUF, h, 0:CH - skip], start=(kt == 0),
                                   stop=(kt == CT * (c + 1) - 1))
                mm.then_inc(pv_made.sem, 1)

            pe.wait_ge(*ones_ok[0])
            pe.wait_ge(*loaded[0][0])
            for n, what in enumerate(ring_start):
                job(what, n, RING + (n + SHIFT) % NRING, n - NRING, 0, -1, len(first) - 1)
            for s in range(AHEAD):
                scores(0, 0, s, 0)
                scores(0, 0, s, 1)

            def unit(u, r, i, more, more2):
                if more:
                    nr, ni = (r + 1) % NPACK, i + (r + 1) // NPACK
                    pe.wait_ge(*loaded[nr][ni])
                n = 0
                for s in range(NS):
                    jobs = (by_step if more else tail)[s]
                    for place in range(3):
                        if place != 1 and s + AHEAD < NS:
                            scores(u, r, s + AHEAD, place // 2)
                        elif place != 1 and more:
                            scores(u + 1, (r + 1) % NPACK, s + AHEAD - NS, place // 2)
                        elif place == 1:
                            values(u, r, s)
                        for what in jobs[len(jobs) * place // 3:len(jobs) * (place + 1) // 3]:
                            job(what, u * J + (J0 + n), bank(n), u * J + (J0 + earlier(n)), (r + 1) % NPACK, u,
                                u * J + (J0 + len(first)))
                            n += 1

            over_units(pe, unit)


def stage_c(nc, shared, woT, x1_scr, o_scr, out):
    ident, causal, ps, neg_half, eps, half_bias, w_ffn, a_all, a_fac, b_fac = shared
    with ExitStack() as ctx:
        every = []

        def sb(name, shape, dt=F32):
            return ctx.enter_context(nc.sbuf_tensor("c_" + name, shape, dt))

        def events(name, step=1, ahead=0):
            every.append(Events(ctx.enter_context(nc.semaphore("c_" + name)), step, ahead))
            return every[-1]

        w_out = [sb(f"w_out{h}", [P, NI, D], F32R) for h in range(2)]
        w_in = sb("w_in", [P, NI, D])
        h_t = sb("h_t", [P, GC, GT * P], F32R)
        o_in = sb("o_in", [P, CT, D])
        x1_in = sb("x1_in", [P, CT, D])
        x2 = sb("x2", [P, CT, D])
        x2_b = sb("x2_b", [P, CT, D])
        x_n = sb("x_n", [P, CT, D])
        x_t = [[sb(f"x_t{n}{h}", [P, NI, CH], F32R) for h in range(2)] for n in range(2)]
        y = sb("y", [P, 2, D])
        stats, moments = sb("stats", [P, CT, 6]), sb("moments", [P, CT, 2])
        var_eps, rstd = sb("var_eps", [P, CT]), sb("rstd", [P, CT])

        w_loaded, w_hi, w_cut = events("w_loaded", 16), events("w_hi"), events("w_cut")
        o_loaded, x1_loaded = events("o_loaded", 16 * CT), events("x1_loaded", 16)
        a_hi, a_cut = events("a_hi"), events("a_cut")
        h_made, h_hi, h_cut = events("h_made"), events("h_hi"), events("h_cut")
        st_ok, mom_ok, var_ok, rstd_ok, norm_ok = [events(s) for s in ("st_ok", "mom_ok", "var_ok", "rstd_ok", "norm_ok")]
        turned, t_hi, t_cut = events("turned"), events("t_hi"), events("t_cut", ahead=2)
        proj_made, proj_taken = events("proj_made", ahead=1), events("proj_taken")
        x2b_made = events("x2b_made")
        ffn_made, ffn_taken = events("ffn_made", ahead=1), events("ffn_taken", ahead=CT)
        y_out = [events(f"y_out{n}", 16, 1) for n in range(2)]

        waited = events("waited")

        block = ctx.enter_context(nc.Block())
        x1_view = x1_scr.rearrange("(t p) d -> p t d", p=P)
        out_view = out.rearrange("(t p) d -> p t d", p=P)

        @block.sync
        def _(sp):
            def load(i, row, half):
                for t in range(CT):
                    src = o_scr[bass.ds(row * NG, NG), bass.ds(half * CH + t * P, P), :].rearrange("g p v -> p g v")
                    sp.dma_start(o_in[:, t, :].rearrange("p (g v) -> p g v", g=NG), src).then_inc(o_loaded.sem, 16)

            load(0, 0, 0)
            sp.dma_start(w_in[:, :, :], woT.rearrange("(c p) d -> p c d", p=P)).then_inc(w_loaded.sem, 16)
            sp.dma_start(x1_in[:, :, :], x1_view[:, 0:CT, :]).then_inc(x1_loaded.sem, 16)
            def chunk(i, last):
                if not last:
                    sp.wait_ge(*turned[i * 2 * CT + CT - 1])
                    load(i + 1, (i + 1) // 2, (i + 1) % 2)
                    sp.wait_ge(*proj_taken[i * CT + CT - 1])
                    sp.dma_start(x1_in[:, :, :], x1_view[:, bass.ds((i + 1) * CT, CT), :]).then_inc(x1_loaded.sem, 16)
                for t in range(CT):
                    sp.wait_ge(*ffn_taken[i * CT + t])
                    sp.dma_start(out_view[:, bass.ds(i * CT + t, 1), :], y[:, t % 2:t % 2 + 1, :]).then_inc(y_out[t % 2].sem, 16)

            with sp.Fori(0, NCH - 1) as i:
                chunk(i, False)
            chunk(NCH - 1, True)
            for n in range(2):
                sp.wait_ge(*y_out[n][NCH * CT // 2 - 1])

        @block.gpsimd
        def _(pool):
            give_ahead(pool, every)
            with pool.Fori(0, NCH) as i:
                for t in range(CT):
                    pool.wait_ge(*mom_ok[i * CT + t])
                    pool.tensor_tensor(var_eps[:, t:t + 1], moments[:, t, 1:2], eps, ALU.add).then_inc(var_ok.sem, 1)
                    pool.wait_ge(*var_ok[i * CT + t])
                    pool.tensor_tensor(rstd[:, t:t + 1], var_eps[:, t:t + 1], neg_half, ALU.pow).then_inc(rstd_ok.sem, 1)
                    pool.wait_ge(*ffn_taken[i * CT + t - CT])
                    pool.tensor_tensor(x2_b[:, t, :], x2[:, t, :], half_bias[:, :], ALU.add).then_inc(x2b_made.sem, 1)

        @block.scalar
        def _(act):
            act.wait_ge(*w_loaded[0])
            act.activation(w_out[0][:, :, :], w_in[:, :, :], ACT.Copy).then_inc(w_hi.sem, 1)

            def turn_hi(i, n):
                act.wait_ge(*turned[i * 2 * CT + n])
                at = n % CT * P
                act.activation(x_t[n // CT][0][:, :, at:at + P], ps[:, 2 + n % 2, :].rearrange("p (c n) -> p c n", c=NI),
                               ACT.Copy).then_inc(t_hi.sem, 1)

            with act.Fori(0, NCH) as i:
                act.wait_ge(*proj_made[i * CT - 1])
                act.wait_ge(*ffn_made[i * CT - 1])
                for n in range(CT):
                    turn_hi(i, n)
                for g in range(GC):
                    group_a_hi(act, a_fac, a_all, g, i * GC + g, a_hi.sem)
                for n in range(CT, 2 * CT):
                    turn_hi(i, n)
                for g in range(GC):
                    act.wait_ge(*h_made[i * GC + g])
                    act.activation(h_t[:, g, :], ps[:, g, 0:GT * P], ACT.Copy).then_inc(h_hi.sem, 1)

        @block.vector
        def _(dve):
            def turn_lo(i, n):
                dve.wait_ge(*t_hi[i * 2 * CT + n])
                at = n % CT * P
                dve.tensor_tensor(x_t[n // CT][1][:, :, at:at + P], ps[:, 2 + n % 2, :].rearrange("p (c n) -> p c n", c=NI),
                                  x_t[n // CT][0][:, :, at:at + P].bitcast(F32), ALU.subtract).then_inc(t_cut.sem, 1)

            def take_ffn(i, t):
                dve.wait_ge(*ffn_made[i * CT + t])
                dve.wait_ge(*x2b_made[i * CT + t])
                dve.wait_ge(*y_out[t % 2][i * (CT // 2) + t // 2 - 1])
                dve.scalar_tensor_tensor(out=y[:, t % 2, :], in0=ps[:, 4 + t, :], scalar=0.5, in1=x2_b[:, t, :],
                                         op0=ALU.mult, op1=ALU.add).then_inc(ffn_taken.sem, 1)

            dve.wait_ge(*w_hi[0])
            dve.tensor_tensor(w_out[1][:, :, :], w_in[:, :, :], w_out[0][:, :, :].bitcast(F32),
                              ALU.subtract).then_inc(w_cut.sem, 1)
            with dve.Fori(0, NCH) as i:
                for t in range(CT):
                    turn_lo(i, t)
                for g in range(GC):
                    dve.wait_ge(*a_hi[i * GC + g])
                    group_a_lo(dve, a_fac, a_all, g, i * GC + g, a_cut.sem)
                dve.wait_ge(*x1_loaded[i])
                for t in range(CT):
                    dve.wait_ge(*proj_made[i * CT + t])
                    dve.tensor_tensor(x2[:, t, :], ps[:, 4 + t, :], x1_in[:, t, :], ALU.add).then_inc(proj_taken.sem, 1)
                    dve.wait_ge(*proj_taken[i * CT + t])
                    dve.bn_stats(stats[:, t, :], x2[:, t, :]).then_inc(st_ok.sem, 1)
                    dve.wait_ge(*st_ok[i * CT + t])
                    dve.sem_inc(waited.sem, 1)
                    dve.bn_aggr(moments[:, t, :], stats[:, t, :]).then_inc(mom_ok.sem, 1)
                    dve.wait_ge(*rstd_ok[i * CT + t])
                    dve.tensor_scalar(x_n[:, t, :], x2[:, t, :], moments[:, t, 0:1], rstd[:, t:t + 1],
                                      ALU.subtract, ALU.mult).then_inc(norm_ok.sem, 1)
                    if t:
                        turn_lo(i, CT + t - 1)
                turn_lo(i, 2 * CT - 1)
                for g in range(GC):
                    dve.wait_ge(*h_hi[i * GC + g])
                    dve.tensor_tensor(h_t[P // 2:P, g, :], ps[P // 2:P, g, 0:GT * P], h_t[P // 2:P, g, :].bitcast(F32),
                                      ALU.subtract).then_inc(h_cut.sem, 1)
                for t in range(CT):
                    take_ffn(i, t)

        @block.tensor
        def _(pe):
            def turn(i, n, source):
                pe.wait_ge(*t_cut[i * 2 * CT + n - 2])
                t = n % CT
                for ic in range(NI):
                    mm = pe.transpose(ps[:, 2 + n % 2, ic * P:(ic + 1) * P], source[:, t, ic * P:(ic + 1) * P], ident[:, :])
                mm.then_inc(turned.sem, 1)

            def ffn_base(i, t):
                pe.wait_ge(*t_cut[i * 2 * CT + CT + t])
                pe.wait_ge(*proj_taken[i * CT + t])
                project(pe, ps[:, 4 + t, :], lambda h, ic: x_t[1][h][:, ic, t * P:(t + 1) * P],
                        lambda h, ic: w_ffn[h][:, ic, :])

            def down(i, g):
                pe.wait_ge(*t_cut[i * 2 * CT + CT + (g + 1) * GT - 1])
                if g == 0:
                    pe.wait_ge(*ffn_made[i * CT - 1])
                pe.wait_ge(*a_cut[i * GC + g])
                low_rank_down(pe, ps[:, g, 0:GT * P], a_fac, x_t[1], g, h_made.sem)

            def up(i, t):
                pe.wait_ge(*h_cut[i * GC + t // GT])
                low_rank_up(pe, ps[:, 4 + t, :], h_t[:, t // GT, t % GT * P:(t % GT + 1) * P], b_fac,
                            i * GC + t // GT, ffn_made.sem)

            with pe.Fori(0, NCH) as i:
                pe.wait_ge(*o_loaded[i])
                for t in range(CT):
                    turn(i, t, o_in)
                pe.wait_ge(*w_cut[0])
                for t in range(CT):
                    pe.wait_ge(*t_cut[i * 2 * CT + t])
                    pe.wait_ge(*ffn_taken[i * CT + t - CT])
                    project(pe, ps[:, 4 + t, :], lambda h, ic: x_t[0][h][:, ic, t * P:(t + 1) * P],
                            lambda h, ic: w_out[h][:, ic, :], proj_made.sem)
                    if t >= 2:
                        pe.wait_ge(*norm_ok[i * CT + t - 2])
                        turn(i, CT + t - 2, x_n)
                ffn_base(i, 0)
                pe.wait_ge(*norm_ok[i * CT + 2])
                turn(i, CT + 2, x_n)
                down(i, 0)
                ffn_base(i, 1)
                pe.wait_ge(*norm_ok[i * CT + 3])
                turn(i, CT + 3, x_n)
                up(i, 0)
                up(i, 1)
                ffn_base(i, 2)
                down(i, 1)
                ffn_base(i, 3)
                up(i, 2)
                up(i, 3)


def kernel(L0_attn_x, L0_attn_Wq, L0_attn_bq, L0_attn_Wk, L0_attn_bk, L0_attn_Wv, L0_attn_bv, L0_attn_Wo,
           L0_attn_bo, L0_ffn_gate, L0_ffn_kernel, L0_ffn_bias, L0_ffn_lora_A, L0_ffn_lora_B,
           L0_ffn_lora_A_shared, L0_ffn_lora_B_shared):
    import numpy as np
    import concourse.bacc as bacc
    from concourse.bass_utils import run_bass_kernel_spmd

    def rows(v):
        return np.broadcast_to(np.asarray(v)[None, :], (P, D))

    shape = np.asarray(L0_attn_x).shape
    arrays = {
        "x": np.asarray(L0_attn_x).reshape(TOK, D),
        "wqT": np.asarray(L0_attn_Wq).T,
        "wkT": np.asarray(L0_attn_Wk).T,
        "wvT": np.asarray(L0_attn_Wv).T,
        "woT": np.asarray(L0_attn_Wo).T,
        "bq": np.asarray(L0_attn_bq).reshape(NI, P).T,
        "bk": np.asarray(L0_attn_bk).reshape(NI, P).T,
        "bv": rows(L0_attn_bv),
        "bo": rows(L0_attn_bo),
        "gate": np.repeat(np.asarray(L0_ffn_gate).T, RANK, axis=0),
        "ffn_w": np.asarray(L0_ffn_kernel),
        "ffn_b": rows(L0_ffn_bias),
        "lora_a": np.asarray(L0_ffn_lora_A).reshape(LORAS * RANK, D),
        "lora_b": np.asarray(L0_ffn_lora_B).transpose(0, 2, 1).reshape(LORAS * RANK, D),
        "lora_as": np.asarray(L0_ffn_lora_A_shared).T,
        "lora_bs": np.asarray(L0_ffn_lora_B_shared).T,
    }
    arrays = {n: np.ascontiguousarray(a) for n, a in arrays.items()}
    nc = bacc.Bacc("TRN2", target_bir_lowering=False, num_devices=1)
    args = [nc.dram_tensor(n, a.shape, mybir.dt.from_np(a.dtype), kind="ExternalInput").ap()
            for n, a in arrays.items()]
    out = nc.dram_tensor("out", (TOK, D), F32, kind="ExternalOutput").ap()
    build(nc, *args, out)
    r = run_bass_kernel_spmd(nc, [arrays], core_ids=[0])
    return r.results[0]["out"].reshape(shape)
```

```python
from contextlib import ExitStack

import concourse.bass as bass
from concourse import mybir

F32 = mybir.dt.float32
F32R = mybir.dt.float32r
BF16 = mybir.dt.bfloat16
ALU = mybir.AluOpType
ACT = mybir.ActivationFunctionType
AX = mybir.AxisListType

P = 128
D = 512
NI = D // P
HD = 16
HEADS = D // HD
TOK = 2048
SEQ = 1024
BATCH = TOK // SEQ
CH = 512
CT = CH // P
NCH = TOK // CH
GROUPS = 8
GT = TOK // GROUPS // P
GC = GROUPS // NCH
LORAS = 16
RANK = 32
LCH = LORAS * RANK // P
EPS = 1e-5
FMIN = -3.0e38

HG = 4
NG = HEADS // HG
UNITS = BATCH * NG
VC = HD + 1
PARTS = 3
TERMS = [(0, 0), (0, 1), (0, 2), (1, 0), (1, 1), (2, 0)]
KROWS = HD * len(TERMS)
SROWS = KROWS + 2
NPACK = 3
LOADS = 3 * len(TERMS) + 1
QT = SEQ // P
STEPS = [(c, kt) for c in range(2) for kt in range(CT * (c + 1))]
NS = len(STEPS)
DIAG = [s for s, (c, kt) in enumerate(STEPS) if kt >= CT * c]
PBUF = 3


class Events:

    def __init__(self, sem, step=1, ahead=0):
        self.sem, self.step, self.ahead = sem, step, ahead

    def __getitem__(self, n):
        return self.sem, (n + (self.ahead + 1)) * self.step


def give_ahead(eng, events):
    for e in events:
        if e.ahead:
            eng.sem_inc(e.sem, e.ahead * e.step)


def project(pe, psum, left, right, done=None):
    terms = [(0, 1), (1, 0), (0, 0)]
    for n, (a, b) in enumerate(terms):
        for ic in range(NI):
            last = pe.matmul(psum, left(a, ic), right(b, ic), start=(n == 0 and ic == 0),
                             stop=(done is not None and n == len(terms) - 1 and ic == NI - 1))
    if done is not None:
        last.then_inc(done, 1)


def low_rank_down(pe, psum, a_fac, x_t, g, done):
    terms = [(0, 1), (1, 0), (0, 0)]
    for n, (a, b) in enumerate(terms):
        for ic in range(NI):
            last = pe.matmul(psum, a_fac[a][:, g, ic, :, :, :].rearrange("p n s r -> p (n s r)"),
                             x_t[b][:, ic, g * GT * P:(g + 1) * GT * P], start=(n == 0 and ic == 0),
                             stop=(n == len(terms) - 1 and ic == NI - 1))
    last.then_inc(done, 1)


def group_a_hi(act, a_fac, a_all, g, group, done):
    src = a_all[:, :, bass.ds(group, 1), :].to_broadcast([P, NI, 2, RANK])
    act.activation(a_fac[0][:, g, :, :, 0, :], src, ACT.Copy).then_inc(done, 1)


def group_a_lo(dve, a_fac, a_all, g, group, done):
    src = a_all[:, :, bass.ds(group, 1), :].to_broadcast([P, NI, 2, RANK])
    dve.tensor_tensor(a_fac[1][:, g, :, :, 0, :], src, a_fac[0][:, g, :, :, 0, :].bitcast(F32),
                      ALU.subtract).then_inc(done, 1)


def low_rank_up(pe, psum, h_t, b_fac, group, done):
    for h in (1, 0):
        last = pe.matmul(psum, h_t, b_fac[h][:, bass.ds(group, 1), :].rearrange("p a d -> p (a d)"),
                         start=False, stop=(h == 0))
    last.then_inc(done, 1)


def unit_pack(nc, ctx, name, n):
    def sb(what, shape, dt):
        return ctx.enter_context(nc.sbuf_tensor(f"{name}_{what}_pack{n}", shape, dt))

    return (sb("q", [SROWS, 2, HG, CH], BF16), sb("k", [SROWS, HG, SEQ], BF16), sb("v", [P, QT, HG * VC], F32))


def unit_loads(u, pack, q_scr, k_scr, v_scr):
    q_pack, k_pack, v_pack = pack
    rows = HG * HD
    loads = []
    for n, (q_part, k_part) in enumerate(TERMS):
        at = slice(n * HD, (n + 1) * HD)
        for c in range(2):
            src = q_scr[q_part, bass.ds(u * rows, rows), c * CH:(c + 1) * CH].rearrange("(h d) n -> d h n", h=HG)
            loads.append((q_pack[at, c, :, :], src))
        src = k_scr[k_part, bass.ds(u * rows, rows), :].rearrange("(h d) n -> d h n", h=HG)
        loads.append((k_pack[at, :, :], src))
    src = v_scr[bass.ds(u, 1), :, :].rearrange("a (t p) v -> p (a t) v", p=P)
    return loads + [(v_pack[:, :, :], src)]


def load_chunk(sp, i, row, half, x1_scr, o_scr, o_in, x1_in, o_loaded, x1_loaded, x1_free=None):
    for t in range(CT):
        src = o_scr[bass.ds(row * NG, NG), bass.ds(half * CH + t * P, P), :].rearrange("g p v -> p g v")
        sp.dma_start(o_in[:, t, :].rearrange("p (g v) -> p g v", g=NG), src).then_inc(o_loaded.sem, 16)
    if x1_free is not None:
        sp.wait_ge(*x1_free)
    src = x1_scr.rearrange("(t p) d -> p t d", p=P)[:, bass.ds(i * CT, CT), :]
    sp.dma_start(x1_in[:, :, :], src).then_inc(x1_loaded.sem, 16)


def build(nc, x, wqT, wkT, wvT, woT, bq, bk, bv, bo, gate, ffn_w, ffn_b, lora_a, lora_b, lora_as, lora_bs, out):
    with ExitStack() as whole:
        def dram(name, shape, dt):
            return nc.dram_tensor(name, shape, dt, kind="Internal").ap()

        def sb(name, shape, dt=F32):
            return whole.enter_context(nc.sbuf_tensor(name, shape, dt))

        b_scr = dram("b_scr", (GROUPS * RANK, D), F32)
        x1_scr = dram("x1_scr", (TOK, D), F32)
        q_scr = dram("q_scr", (PARTS, BATCH * D, SEQ), BF16)
        k_scr = dram("k_scr", (PARTS, BATCH * D, SEQ), BF16)
        v_scr = dram("v_scr", (UNITS, SEQ, HG * VC), F32)
        o_scr = dram("o_scr", (UNITS, SEQ, HG * HD), F32)

        with ExitStack() as raw:
            w_ffn_raw = raw.enter_context(nc.sbuf_tensor("w_ffn_raw", [P, NI, D], F32))
            b_raw = raw.enter_context(nc.sbuf_tensor("b_raw", [P, GROUPS, D], F32))
        w_ffn_lo = sb("w_ffn_lo", [P, NI, D], F32R)
        b_lo = sb("b_lo", [P, GROUPS, D], F32R)
        w_ffn, b_fac = [sb("w_ffn_hi", [P, NI, D], F32R), w_ffn_lo], [sb("b_hi", [P, GROUPS, D], F32R), b_lo]
        ident = sb("ident", [P, P])
        causal = sb("causal", [P, CH])
        ps = whole.enter_context(nc.psum_tensor("ps", [P, 8, 512], F32))
        small = sb("small", [P, 8])
        neg_half, eps = small[:, 0:1], small[:, 1:2]
        half_bias = sb("half_bias", [P, D])
        a_all = sb("a_all", [P, NI, GROUPS, RANK])
        a_fac = [sb(f"a_fac{h}", [P, GC, NI, 2, 2, RANK], F32R) for h in range(2)]
        with ExitStack() as early:
            pack0 = unit_pack(nc, early, "early", 0)
        loaded0 = Events(whole.enter_context(nc.semaphore("loaded0")), 16 * LOADS)
        shared = (ident, causal, ps, neg_half, eps, half_bias, w_ffn, a_all, a_fac, b_fac)

        stage_a(nc, shared, w_ffn_raw, b_raw, x, wqT, wkT, wvT, bq, bk, bv, bo, gate, ffn_w, ffn_b, lora_a, lora_b,
                lora_as, lora_bs, b_scr, x1_scr, q_scr, k_scr, v_scr, pack0, loaded0)
        unit_pack(nc, whole, "place_of", 0)
        with ExitStack() as raw:
            w_out_raw = raw.enter_context(nc.sbuf_tensor("w_out_raw", [P, NI, D], F32))
        w_out = [sb(f"w_out_{s}", [P, NI, D], F32R) for s in ("lo", "hi")][::-1]
        o_in = sb("o_in", [P, CT, D])
        x1_in = sb("x1_in", [P, CT, D])
        w_loaded, w_hi, w_cut, o_loaded, x1_loaded = [Events(whole.enter_context(nc.semaphore(name)), step) for name, step in (
            ("w_out_loaded", 16), ("w_out_hi", 1), ("w_out_cut", 1), ("o_loaded", 16 * CT), ("x1_loaded", 16))]
        start_c = (w_out_raw, w_out, o_in, x1_in, w_loaded, w_hi, w_cut, o_loaded, x1_loaded)

        stage_b(nc, ps, ident, causal, q_scr, k_scr, v_scr, o_scr, pack0, loaded0, woT, x1_scr, start_c)
        stage_c(nc, shared, x1_scr, o_scr, out, start_c)


def stage_a(nc, shared, w_ffn_raw, b_raw, x, wqT, wkT, wvT, bq, bk, bv, bo, gate, ffn_w, ffn_b, lora_a, lora_b,
            lora_as, lora_bs, b_scr, x1_scr, q_scr, k_scr, v_scr, pack0, loaded0):
    ident, causal, ps, neg_half, eps, half_bias, w_ffn, a_all, a_fac, b_fac = shared
    with ExitStack() as ctx:
        every = []
        QKBUF = 4

        def sb(name, shape, dt=F32):
            return ctx.enter_context(nc.sbuf_tensor("a_" + name, shape, dt))

        def events(name, step=1, ahead=0):
            every.append(Events(ctx.enter_context(nc.semaphore("a_" + name)), step, ahead))
            return every[-1]

        with ExitStack() as raw:
            w_v_raw = raw.enter_context(nc.sbuf_tensor("a_w_v_raw", [P, NI, D], F32))
        w_v = [sb(f"w_v_{s}", [P, NI, D], F32R) for s in ("lo", "hi")][::-1]
        with ExitStack() as raw:
            w_raw = [raw.enter_context(nc.sbuf_tensor(f"a_w_{n}_raw", [P, NI, D], F32)) for n in "qk"] + [w_v_raw]
            lora_ab = [raw.enter_context(nc.sbuf_tensor(f"adapters_{n}", [P, LCH, D], F32)) for n in "ab"]
        w_lo = [sb(f"w_{n}_lo", [P, NI, D], F32R) for n in "qk"]
        w_qkv = [[sb(f"w_{n}_hi", [P, NI, D], F32R), w_lo["qk".index(n)]] for n in "qk"] + [w_v]
        x_in = sb("x_in", [P, CT, D])
        x_n = sb("x_n", [P, CT, D])
        x_t = [sb(f"x_t{h}", [P, NI, CH], F32R) for h in range(2)]
        x1 = sb("x1", [P, CT, D])
        h_t = sb("h_t", [P, GC, GT * P], F32R)
        x1_b = sb("x1_b", [P, 2, D])
        stats, moments = sb("stats", [P, 2, CT, 6]), sb("moments", [P, 2, CT, 2])
        var_eps, rstd = sb("var_eps", [P, 2, CT]), sb("rstd", [P, 2, CT])
        qk = sb("qk", [P, QKBUF, CH])
        rest = sb("rest", [P, QKBUF, CH])
        parts = sb("parts", [P, QKBUF, PARTS, CH], BF16)
        v_tile = sb("v_tile", [P, 2, HEADS, VC])
        biases = sb("biases", [P, 2, D])
        b_qk = sb("b_qk", [P, 2, NI])
        gate_rows = sb("gate_rows", [P, LCH, GROUPS])
        delta = sb("delta", [P, RANK])
        spread = sb("spread", [P, LCH, GROUPS, RANK])
        as_in = sb("as_in", [P, NI, RANK])

        gate_in, adapters_in, as_loaded = events("gate_in", 16), [events("a_in", 16), events("b_in", 16)], events("as_in", 16)
        zeroed, spread_ok = events("zeroed"), events("spread_ok")
        down_made, down_taken = events("down_made"), events("down_taken")
        shared_hi, shared_cut = events("shared_hi"), events("shared_cut")
        a_hi, a_cut = events("a_hi"), events("a_cut")
        up_made, up_taken, up_out = events("up_made"), events("up_taken"), events("up_out", 16)
        b_loaded = events("b_loaded", 16 * 4)
        b_hi, b_cut = events("b_hi"), events("b_cut")
        wf_loaded, wf_hi, wf_cut = events("wf_loaded", 16), events("wf_hi"), events("wf_cut")
        w_loaded, w_hi, w_cut = [[events(f"w{n}_{s}", c) for n in range(3)] for s, c in (("loaded", 16), ("hi", 1), ("cut", 1))]
        params_in = events("params_in", 16 * 5)
        consts, scaled = events("consts"), events("scaled")
        x_loaded, xb_made = [events(f"x_loaded{t}", 16) for t in range(CT)], events("xb_made")
        st_ok, mom_ok, var_ok, rstd_ok, norm_ok = [[events(f"{s}{n}") for n in range(2)] for s in
                                                   ("st_ok", "mom_ok", "var_ok", "rstd_ok", "norm_ok")]
        turned, t_hi, t_cut = events("turned"), events("t_hi"), events("t_cut", ahead=2)
        h_made, h_hi, h_cut = events("h_made"), events("h_hi"), events("h_cut")
        ffn_made, ffn_taken = events("ffn_made", ahead=1), events("ffn_taken")
        v_made, v_taken = events("v_made"), events("v_taken")
        v_out = [events(f"v_out{n}", 16, 1) for n in range(2)]
        qk_made, qk_taken = events("qk_made", ahead=1), events("qk_taken", ahead=CT)
        part1, rest_ok, part2, qk_cut = events("part1"), events("rest_ok"), events("part2"), events("qk_cut", ahead=QKBUF)
        parts_out = [events(f"parts_out{n}", 16, 1) for n in range(QKBUF)]
        x1b_made, x1_out = events("x1b_made", ahead=CT), [events(f"x1_out{n}", 16, 1) for n in range(2)]

        waited = events("waited")

        block = ctx.enter_context(nc.Block())
        x_view = x.rearrange("(t p) d -> p t d", p=P)
        x1_view = x1_scr.rearrange("(t p) d -> p t d", p=P)

        @block.sync
        def _(sp):
            def load_x(tile, t):
                sp.dma_start(x_in[:, t:t + 1, :], x_view[:, bass.ds(tile, 1), :]).then_inc(x_loaded[t].sem, 16)

            def load_rows(dst, src, signal):
                sp.dma_start(dst, src.rearrange("(c p) d -> p c d", p=P)).then_inc(signal.sem, 16)

            sp.dma_start(gate_rows[:, :, :], gate.rearrange("(c p) b -> p c b", p=P)).then_inc(gate_in.sem, 16)
            load_x(0, 0)
            load_rows(lora_ab[0][:, :, :], lora_a, adapters_in[0])
            for t in range(1, CT):
                load_x(t, t)
            sp.dma_start(as_in[:, :, :], lora_as.rearrange("(c p) r -> p c r", p=P)).then_inc(as_loaded.sem, 16)
            load_rows(w_ffn_raw[:, :, :], ffn_w, wf_loaded)
            load_rows(lora_ab[1][:, :, :], lora_b, adapters_in[1])
            for dst, src in ((half_bias[:, :], ffn_b), (biases[:, 0, :], bv), (biases[:, 1, :], bo),
                             (b_qk[:, 0, :], bq), (b_qk[:, 1, :], bk)):
                sp.dma_start(dst, src).then_inc(params_in.sem, 16)
            for at in (RANK, 3 * RANK):
                sp.dma_start(b_raw[at:at + RANK, :, :],
                             lora_bs.unsqueeze(1).to_broadcast([RANK, GROUPS, D])).then_inc(b_loaded.sem, 16)
            load_rows(w_raw[2][:, :, :], wvT, w_loaded[2])
            for half in range(2):
                sp.wait_ge(*up_taken[half])
                sp.dma_start(b_scr[half * P:(half + 1) * P, :], x1[:, half, :]).then_inc(up_out.sem, 16)
            sp.wait_ge(*up_out[1])
            for at in (0, 2 * RANK):
                sp.dma_start(b_raw[at:at + RANK, :, :],
                             b_scr.rearrange("(b r) d -> r b d", r=RANK)).then_inc(b_loaded.sem, 16)
            load_rows(w_raw[0][:, :, :], wqT, w_loaded[0])
            load_rows(w_raw[1][:, :, :], wkT, w_loaded[1])

            def chunk(i, last):
                row, half = i // 2, i % 2
                for t in range(CT):
                    if not last:
                        sp.wait_ge(*ffn_taken[i * CT + t])
                        load_x((i + 1) * CT + t, t)
                    sp.wait_ge(*x1b_made[i * CT + t])
                    sp.dma_start(x1_view[:, bass.ds(i * CT + t, 1), :],
                                 x1_b[:, t % 2:t % 2 + 1, :]).then_inc(x1_out[t % 2].sem, 16)
                for t in range(CT):
                    sp.wait_ge(*v_taken[i * CT + t])
                    dst = v_scr[bass.ds(row * NG, NG), bass.ds(half * CH + t * P, P), :].rearrange("g p v -> p g v")
                    src = v_tile[:, t % 2, :, :].rearrange("p (g h) v -> p g (h v)", g=NG)
                    sp.dma_start(dst, src).then_inc(v_out[t % 2].sem, 16)
                if last:
                    early = unit_loads(0, pack0, q_scr, k_scr, v_scr)
                    for n in range(2):
                        sp.wait_ge(*v_out[n][NCH // BATCH * CT // 2 - 1])
                    for out in parts_out:
                        sp.wait_ge(*out[NCH // BATCH * 2 * NI // QKBUF - 1])
                for j in range(2 * NI):
                    scr = (q_scr, k_scr)[j // NI]
                    sp.wait_ge(*qk_cut[i * 2 * NI + j])
                    dst = scr[:, bass.ds(row * D + (j % NI) * P, P), bass.ds(half * CH, CH)].rearrange("s p n -> p s n")
                    sp.dma_start(dst, parts[:, j % QKBUF, :, :]).then_inc(parts_out[j % QKBUF].sem, 16)
                    if last:
                        for dst, src in early[3 * j:3 * j + 3]:
                            sp.dma_start(dst, src).then_inc(loaded0.sem, 16)

            with sp.Fori(0, NCH - 1) as i:
                chunk(i, False)
            chunk(NCH - 1, True)
            for n in range(2):
                sp.wait_ge(*x1_out[n][NCH * CT // 2 - 1])
                sp.wait_ge(*v_out[n][NCH * CT // 2 - 1])
            for out in parts_out:
                sp.wait_ge(*out[NCH * 2 * NI // QKBUF - 1])

        @block.gpsimd
        def _(pool):
            give_ahead(pool, every)
            pool.memset(delta[:, :], 0.0).then_inc(zeroed.sem, 1)
            for n in range(P // RANK):
                pool.wait_ge(*zeroed[n])
                pool.affine_select(out=delta[:, :], in_=delta[:, :], compare_op=ALU.not_equal, fill=1.0,
                                   base=-n * RANK, pattern=[[-1, RANK]], channel_multiplier=1).then_inc(zeroed.sem, 1)
            pool.memset(neg_half, -0.5).then_inc(consts.sem, 1)
            pool.memset(eps, EPS).then_inc(consts.sem, 1)
            pool.memset(ident[:, :], 0.0).then_inc(consts.sem, 1)
            pool.memset(causal[:, :], 0.0).then_inc(consts.sem, 1)
            pool.wait_ge(*consts[3])
            pool.affine_select(out=ident[:, :], in_=ident[:, :], compare_op=ALU.not_equal, fill=1.0, base=0,
                               pattern=[[-1, P]], channel_multiplier=1).then_inc(consts.sem, 1)
            pool.affine_select(out=causal[:, CH - P:CH], in_=causal[:, CH - P:CH], compare_op=ALU.is_ge,
                               fill=FMIN, base=0, pattern=[[-1, P]], channel_multiplier=1).then_inc(consts.sem, 1)
            pool.memset(v_tile[:, :, :, HD:VC], 1.0).then_inc(consts.sem, 1)

            def rstd_of(ln, i, t):
                pool.wait_ge(*mom_ok[ln][i * CT + t])
                pool.tensor_tensor(var_eps[:, ln, t:t + 1], moments[:, ln, t, 1:2], eps, ALU.add).then_inc(var_ok[ln].sem, 1)
                pool.wait_ge(*var_ok[ln][i * CT + t])
                pool.tensor_tensor(rstd[:, ln, t:t + 1], var_eps[:, ln, t:t + 1], neg_half,
                                   ALU.pow).then_inc(rstd_ok[ln].sem, 1)

            def add_bias(i, t):
                pool.wait_ge(*norm_ok[0][i * CT + t])
                pool.tensor_tensor(x_in[:, t, :], x_in[:, t, :], half_bias[:, :], ALU.add).then_inc(xb_made.sem, 1)

            def store_x1(i, t):
                pool.wait_ge(*ffn_taken[i * CT + t])
                pool.wait_ge(*x1_out[t % 2][i * (CT // 2) + t // 2 - 1])
                pool.tensor_tensor(x1_b[:, t % 2, :], x1[:, t, :], biases[:, 1, :], ALU.add).then_inc(x1b_made.sem, 1)

            def chunk(i, last):
                for t in range(CT):
                    rstd_of(1, i, t)
                    if t:
                        store_x1(i, t - 1)
                store_x1(i, CT - 1)
                if not last:
                    for t in range(CT):
                        rstd_of(0, i + 1, t)
                    for t in range(CT):
                        add_bias(i + 1, t)

            for t in range(CT):
                rstd_of(0, 0, t)
            pool.wait_ge(*params_in[0])
            pool.tensor_scalar(half_bias[:, :], half_bias[:, :], 0.5, None, ALU.mult).then_inc(scaled.sem, 1)
            pool.tensor_scalar(b_qk[:, 0, :], b_qk[:, 0, :], float(HD) ** -0.5, None, ALU.mult).then_inc(scaled.sem, 1)
            pool.wait_ge(*scaled[0])
            for t in range(CT):
                add_bias(0, t)
            with pool.Fori(0, NCH - 1) as i:
                chunk(i, False)
            chunk(NCH - 1, True)

        @block.scalar
        def _(act):
            def turn_hi(i, n):
                act.wait_ge(*turned[i * 2 * CT + n])
                if n >= CT:
                    act.wait_ge(*ffn_made[i * CT + n - CT])
                at = n % CT * P
                act.activation(x_t[0][:, :, at:at + P], ps[:, 2 + n % 2, :].rearrange("p (c n) -> p c n", c=NI),
                               ACT.Copy).then_inc(t_hi.sem, 1)

            def second_part(i, j):
                act.wait_ge(*rest_ok[i * 2 * NI + j])
                act.activation(parts[:, j % QKBUF, 1, :], rest[:, j % QKBUF, :], ACT.Copy).then_inc(part2.sem, 1)

            def weights(n):
                act.wait_ge(*w_loaded[n][0])
                if n < 2:
                    for half in range(2):
                        act.wait_ge(*up_made[half])
                act.activation(w_qkv[n][0][:, :, :], w_raw[n][:, :, :], ACT.Copy).then_inc(w_hi[n].sem, 1)

            def first_turns(i):
                act.wait_ge(*qk_made[i * 2 * NI - 1])
                turn_hi(i, 0)
                turn_hi(i, 1)

            def chunk(i, first, last):
                turn_hi(i, 2)
                turn_hi(i, 3)
                for g in range(GC):
                    group_a_hi(act, a_fac, a_all, g, i * GC + g, a_hi.sem)
                if first:
                    act.wait_ge(*b_loaded[0])
                for g in range(GC):
                    group = bass.ds(i * GC + g, 1)
                    act.activation(b_fac[0][:, group, :], b_raw[:, group, :], ACT.Copy).then_inc(b_hi.sem, 1)
                for g in range(GC):
                    act.wait_ge(*h_made[i * GC + g])
                    act.wait_ge(*ffn_made[i * CT - 1])
                    act.activation(h_t[:, g, :], ps[:, g, 0:GT * P], ACT.Copy).then_inc(h_hi.sem, 1)
                if first:
                    weights(2)
                turn_hi(i, CT)
                turn_hi(i, CT + 1)
                if first:
                    weights(0)
                turn_hi(i, CT + 2)
                turn_hi(i, CT + 3)
                if first:
                    weights(1)
                    act.wait_ge(*scaled[1])
                for j in range(2 * NI):
                    kq, n = j // NI, i * 2 * NI + j
                    act.wait_ge(*qk_made[n])
                    act.wait_ge(*qk_cut[n - QKBUF])
                    act.activation(qk[:, j % QKBUF, :], ps[:, 4 + j % 4, :], ACT.Identity,
                                   bias=b_qk[:, kq, j % NI:j % NI + 1],
                                   scale=(float(HD) ** -0.5, 1.0)[kq]).then_inc(qk_taken.sem, 1)
                    if not last and j == 2 * NI - 1:
                        first_turns(i + 1)
                    if j:
                        second_part(i, j - 1)
                    act.wait_ge(*qk_taken[n])
                    act.wait_ge(*parts_out[j % QKBUF][i * (2 * NI // QKBUF) + j // QKBUF - 1])
                    act.activation(parts[:, j % QKBUF, 0, :], qk[:, j % QKBUF, :], ACT.Copy).then_inc(part1.sem, 1)
                second_part(i, 2 * NI - 1)

            act.wait_ge(*as_loaded[0])
            for g in range(GC):
                act.activation(a_fac[0][:, g, :, :, 1, :], as_in[:, :, :].unsqueeze(2).to_broadcast([P, NI, 2, RANK]),
                               ACT.Copy).then_inc(shared_hi.sem, 1)
            for ic in range(NI):
                act.wait_ge(*down_made[ic])
                act.activation(a_all[:, ic, :, :], ps[:, ic, 0:GROUPS * RANK].rearrange("p (b r) -> p b r", b=GROUPS),
                               ACT.Copy).then_inc(down_taken.sem, 1)
            act.wait_ge(*down_taken[NI - 1])
            act.wait_ge(*wf_loaded[0])
            for ic in range(NI):
                act.activation(w_ffn[0][:, ic, :], w_ffn_raw[:, ic, :], ACT.Copy).then_inc(wf_hi.sem, 1)
            first_turns(0)
            chunk(0, True, False)
            with act.Fori(1, NCH - 1) as i:
                chunk(i, False, False)
            chunk(NCH - 1, False, True)

        @block.vector
        def _(dve):
            def norm(ln, i, t, rows):
                dve.bn_stats(stats[:, ln, t, :], rows).then_inc(st_ok[ln].sem, 1)
                dve.wait_ge(*st_ok[ln][i * CT + t])
                dve.sem_inc(waited.sem, 1)
                dve.bn_aggr(moments[:, ln, t, :], stats[:, ln, t, :]).then_inc(mom_ok[ln].sem, 1)

            def norm_out(ln, i, t, rows):
                dve.wait_ge(*rstd_ok[ln][i * CT + t])
                dve.tensor_scalar(x_n[:, t, :], rows, moments[:, ln, t, 0:1], rstd[:, ln, t:t + 1],
                                  ALU.subtract, ALU.mult).then_inc(norm_ok[ln].sem, 1)

            def turn_lo(i, n):
                dve.wait_ge(*t_hi[i * 2 * CT + n])
                at = n % CT * P
                dve.tensor_tensor(x_t[1][:, :, at:at + P], ps[:, 2 + n % 2, :].rearrange("p (c n) -> p c n", c=NI),
                                  x_t[0][:, :, at:at + P].bitcast(F32), ALU.subtract).then_inc(t_cut.sem, 1)

            def lo_part(pair, raw, *at):
                return dve.tensor_tensor(pair[1][at], raw[at], pair[0][at].bitcast(F32), ALU.subtract)

            def weights(n):
                dve.wait_ge(*w_hi[n][0])
                lo_part(w_qkv[n], w_raw[n], slice(None), slice(None), slice(None)).then_inc(w_cut[n].sem, 1)

            def third_part(i, j):
                dve.wait_ge(*part2[i * 2 * NI + j])
                dve.tensor_tensor(parts[:, j % QKBUF, 2, :], rest[:, j % QKBUF, :], parts[:, j % QKBUF, 1, :],
                                  ALU.subtract).then_inc(qk_cut.sem, 1)

            def ffn_sum(i, t):
                dve.wait_ge(*ffn_made[i * CT + t])
                dve.wait_ge(*xb_made[i * CT + t])
                dve.wait_ge(*x1b_made[i * CT + t - CT])
                dve.scalar_tensor_tensor(out=x1[:, t, :], in0=ps[:, 4 + t, :], scalar=0.5, in1=x_in[:, t, :],
                                         op0=ALU.mult, op1=ALU.add).then_inc(ffn_taken.sem, 1)
                dve.wait_ge(*ffn_taken[i * CT + t])
                norm(1, i, t, x1[:, t, :])

            def v_sum(i, t):
                dve.wait_ge(*v_made[i * CT + t])
                dve.wait_ge(*v_out[t % 2][i * (CT // 2) + t // 2 - 1])
                dve.tensor_tensor(v_tile[:, t % 2, :, 0:HD], ps[:, 4 + t, :].rearrange("p (h d) -> p h d", h=HEADS),
                                  biases[:, 0, :].rearrange("p (h d) -> p h d", h=HEADS), ALU.add).then_inc(v_taken.sem, 1)

            def low_h(i, g):
                dve.wait_ge(*h_hi[i * GC + g])
                dve.tensor_tensor(h_t[P // 2:P, g, :], ps[P // 2:P, g, 0:GT * P], h_t[P // 2:P, g, :].bitcast(F32),
                                  ALU.subtract).then_inc(h_cut.sem, 1)

            def chunk(i, first, last):
                turn_lo(i, 2)
                turn_lo(i, 3)
                for g in range(GC):
                    dve.wait_ge(*a_hi[i * GC + g])
                    group_a_lo(dve, a_fac, a_all, g, i * GC + g, a_cut.sem)
                for g in range(GC):
                    dve.wait_ge(*b_hi[i * GC + g])
                    lo_part(b_fac, b_raw, slice(None), bass.ds(i * GC + g, 1), slice(None)).then_inc(b_cut.sem, 1)
                low_h(i, 0)
                low_h(i, 1)
                if first:
                    dve.wait_ge(*up_out[1])
                ffn_sum(i, 0)
                ffn_sum(i, 1)
                norm_out(1, i, 0, x1[:, 0, :])
                norm_out(1, i, 1, x1[:, 1, :])
                if first:
                    weights(2)
                turn_lo(i, CT)
                ffn_sum(i, 2)
                turn_lo(i, CT + 1)
                norm_out(1, i, 2, x1[:, 2, :])
                ffn_sum(i, 3)
                norm_out(1, i, 3, x1[:, 3, :])
                v_sum(i, 0)
                turn_lo(i, CT + 2)
                v_sum(i, 1)
                turn_lo(i, CT + 3)
                if first:
                    weights(0)
                v_sum(i, 2)
                v_sum(i, 3)
                if first:
                    weights(1)
                for j in range(2 * NI):
                    if not last and j == 2 * NI - 1:
                        turn_lo(i + 1, 0)
                        turn_lo(i + 1, 1)
                    dve.wait_ge(*part1[i * 2 * NI + j])
                    dve.tensor_tensor(rest[:, j % QKBUF, :], qk[:, j % QKBUF, :], parts[:, j % QKBUF, 0, :],
                                      ALU.subtract).then_inc(rest_ok.sem, 1)
                    if j:
                        third_part(i, j - 1)
                    if not last and j < CT:
                        dve.wait_ge(*x_loaded[j][i + 1])
                        norm(0, i + 1, j, x_in[:, j, :])
                    if not last and 2 <= j < CT + 2:
                        norm_out(0, i + 1, j - 2, x_in[:, j - 2, :])
                third_part(i, 2 * NI - 1)

            dve.wait_ge(*zeroed[P // RANK])
            dve.wait_ge(*gate_in[0])
            for c in range(LCH):
                dve.tensor_tensor(spread[:, c, :, :],
                                  delta[:, :].unsqueeze(1).to_broadcast([P, GROUPS, RANK]),
                                  gate_rows[:, c, :].unsqueeze(2).to_broadcast([P, GROUPS, RANK]),
                                  ALU.mult).then_inc(spread_ok.sem, 1)
            for t in range(CT):
                dve.wait_ge(*x_loaded[t][0])
                norm(0, 0, t, x_in[:, t, :])
            for t in range(CT):
                norm_out(0, 0, t, x_in[:, t, :])
            for g in range(GC):
                dve.wait_ge(*shared_hi[g])
                dve.tensor_tensor(a_fac[1][:, g, :, :, 1, :], as_in[:, :, :].unsqueeze(2).to_broadcast([P, NI, 2, RANK]),
                                  a_fac[0][:, g, :, :, 1, :].bitcast(F32), ALU.subtract).then_inc(shared_cut.sem, 1)
            for ic in range(NI):
                dve.wait_ge(*wf_hi[ic])
                lo_part(w_ffn, w_ffn_raw, slice(None), ic, slice(None)).then_inc(wf_cut.sem, 1)
            for half in range(2):
                dve.wait_ge(*up_made[half])
                dve.tensor_copy(x1[:, half, :], ps[:, 6 + half, :]).then_inc(up_taken.sem, 1)
            dve.wait_ge(*consts[6])
            dve.wait_ge(*params_in[0])
            turn_lo(0, 0)
            turn_lo(0, 1)
            chunk(0, True, False)
            with dve.Fori(1, NCH - 1) as i:
                chunk(i, False, False)
            chunk(NCH - 1, False, True)

        @block.tensor
        def _(pe):
            def turn(i, n):
                ln, t = n // CT, n % CT
                pe.wait_ge(*norm_ok[ln][i * CT + t])
                pe.wait_ge(*t_cut[i * 2 * CT + n - 2])
                for ic in range(NI):
                    mm = pe.transpose(ps[:, 2 + n % 2, ic * P:(ic + 1) * P], x_n[:, t, ic * P:(ic + 1) * P], ident[:, :])
                mm.then_inc(turned.sem, 1)

            def rows(t):
                return lambda h, ic: x_t[h][:, ic, t * P:(t + 1) * P]

            def ffn_base(i, t):
                pe.wait_ge(*t_cut[i * 2 * CT + t])
                pe.wait_ge(*qk_taken[i * 2 * NI - CT + t])
                if t >= 2:
                    pe.wait_ge(*up_taken[t - 2])
                project(pe, ps[:, 4 + t, :], rows(t), lambda h, ic: w_ffn[h][:, ic, :])

            def down(i, g):
                pe.wait_ge(*t_cut[i * 2 * CT + (g + 1) * GT - 1])
                pe.wait_ge(*a_cut[i * GC + g])
                low_rank_down(pe, ps[:, g, 0:GT * P], a_fac, x_t, g, h_made.sem)

            def up(i, t):
                g = t // GT
                pe.wait_ge(*h_cut[i * GC + g])
                pe.wait_ge(*b_cut[i * GC + g])
                low_rank_up(pe, ps[:, 4 + t, :], h_t[:, g, t % GT * P:(t % GT + 1) * P], b_fac, i * GC + g, ffn_made.sem)

            def v_rows(i, t):
                pe.wait_ge(*t_cut[i * 2 * CT + CT + t])
                pe.wait_ge(*ffn_taken[i * CT + t])
                pe.wait_ge(*w_cut[2][0])
                project(pe, ps[:, 4 + t, :], rows(t), lambda h, ic: w_qkv[2][h][:, ic, :], v_made.sem)

            pe.wait_ge(*spread_ok[LCH - 1])
            pe.wait_ge(*adapters_in[0][0])
            for ic in range(NI):
                for c in range(LCH):
                    mm = pe.matmul(ps[:, ic, 0:GROUPS * RANK], lora_ab[0][:, c, ic * P:(ic + 1) * P],
                                   spread[:, c, :, :].rearrange("p b r -> p (b r)"), start=(c == 0), stop=(c == LCH - 1))
                mm.then_inc(down_made.sem, 1)
            pe.wait_ge(*adapters_in[1][0])
            for half in range(2):
                for c in range(LCH):
                    g = spread[:, c, half * GROUPS // 2:(half + 1) * GROUPS // 2, :].rearrange("p b r -> p (b r)")
                    mm = pe.matmul(ps[:, 6 + half, :], g, lora_ab[1][:, c, :], start=(c == 0), stop=(c == LCH - 1))
                mm.then_inc(up_made.sem, 1)
            pe.wait_ge(*consts[4])
            pe.wait_ge(*shared_cut[GC - 1])
            pe.wait_ge(*down_taken[NI - 1])
            pe.wait_ge(*wf_cut[NI - 1])

            def chunk(i):
                turn(i, 0)
                turn(i, 1)
                ffn_base(i, 0)
                turn(i, 2)
                turn(i, 3)
                ffn_base(i, 1)
                down(i, 0)
                down(i, 1)
                up(i, 0)
                up(i, 1)
                ffn_base(i, 2)
                ffn_base(i, 3)
                turn(i, CT)
                up(i, 2)
                up(i, 3)
                turn(i, CT + 1)
                v_rows(i, 0)
                turn(i, CT + 2)
                v_rows(i, 1)
                turn(i, CT + 3)
                v_rows(i, 2)
                v_rows(i, 3)
                for j in range(2 * NI):
                    at = j % NI * P
                    if j < CT:
                        pe.wait_ge(*v_taken[i * CT + j])
                    else:
                        pe.wait_ge(*qk_taken[i * 2 * NI + j - CT])
                    pe.wait_ge(*w_cut[j // NI][0])
                    project(pe, ps[:, 4 + j % 4, :], lambda h, ic: w_qkv[j // NI][h][:, ic, at:at + P],
                            lambda h, ic: x_t[h][:, ic, :], qk_made.sem)

            with pe.Fori(0, NCH) as i:
                chunk(i)


def score_jobs():
    first = [("max", 0, h, q, 0, (q + 1) * P) for q in range(CT) for h in range(HG)]
    second = []
    for q in range(CT):
        for h in range(HG):
            second += [("max", 1, h, q, 0, CH), ("max", 1, h, q, CH, (q + 1) * P)]
    return first, second


def stage_b(nc, ps, ident, causal, q_scr, k_scr, v_scr, o_scr, pack0, loaded0, woT, x1_scr, start_c):
    w_out_raw, w_out, o_in, x1_in, w_loaded, w_hi, w_cut, o_loaded, x1_loaded = start_c
    with ExitStack() as ctx:
        every = []

        def sb(name, shape, dt=F32):
            return ctx.enter_context(nc.sbuf_tensor("b_" + name, shape, dt))

        def events(name, step=1, ahead=0):
            every.append(Events(ctx.enter_context(nc.semaphore("b_" + name)), step, ahead))
            return every[-1]

        S_BANK, O_BANK, RING, NRING = 0, 4, 5, 3
        AHEAD = 2

        packs = [pack0] + [unit_pack(nc, ctx, "b", n) for n in range(1, NPACK)]
        q_pack, k_pack, v_pack = zip(*packs)
        probs = sb("probs", [P, PBUF, HG, CH])
        top = sb("top", [P, 4, HG * CT])
        neg_top = sb("neg_top", [HG * CT, 2, 2, P], BF16)
        o_t = sb("o_t", [P, 2, CH])
        inv = sb("inv", [P, 2, HG * CT])
        o_rows = sb("o_rows", [P, 2, HG * CT, HD])

        def width(s):
            c, kt = STEPS[s]
            return CH - max(0, kt - CT * c) * P

        first, second = score_jobs()
        ring_start = first + [("turn", 0)] + second
        J0 = len(ring_start)

        def weight(s):
            return width(s) + 0.7 * width((s + AHEAD) % NS)

        def jobs_by_step():
            todo = first + [("turn", 0)] + second
            cost = [75 + (job[5] if job[0] == "max" else P) for job in todo]
            all_cost, all_width = sum(cost), sum(map(weight, range(NS)))
            by_step, given = [], 0.0
            for s in range(NS):
                now = [("turn", 1)] if s == 0 else []
                goal = all_cost * sum(map(weight, range(s + 1))) / all_width
                while todo and given + cost[0] / 2 <= goal:
                    now.append(todo.pop(0))
                    given += cost.pop(0)
                if s == CT:
                    now.append(("out", 0))
                by_step.append(now)
            return by_step[:-1] + [by_step[-1] + todo + [("out", 1)]]

        by_step = jobs_by_step()
        ring = sum(by_step, [])
        J = len(ring)
        tail = [[("turn", 1)] if s == 0 else [("out", 0)] if s == CT else [("out", 1)] if s == NS - 1 else []
                for s in range(NS)]

        EMPTY = (17, 48)
        slot = [n + sum(n >= e for e in EMPTY) for n in range(J)]
        SLOTS = J + len(EMPTY)
        SHIFT = -J0 % NRING
        assert SLOTS % NRING == 0

        def bank(n):
            return RING + slot[n] % NRING

        def earlier(n):
            s = slot[n]
            while True:
                s -= NRING
                if s < 0:
                    return slot.index(s + SLOTS) - J
                if s in slot:
                    return slot.index(s)

        def ring_of(more):
            return ring if more else sum(tail, [])

        loaded = [loaded0] + [events(f"loaded{n}", 16 * LOADS) for n in range(1, NPACK)]
        ones_ok = events("ones_ok", NPACK + 1)
        ring_made, ring_taken = events("ring_made"), events("ring_taken", ahead=NRING)
        top_ok, neg_hi = events("top_ok"), events("neg_hi")
        neg_in = [events(f"neg_in{c}", 32, 1) for c in range(2)]
        s_made, s_taken = events("s_made"), events("s_taken", ahead=2)
        masked = events("masked")
        pv_made = events("pv_made", ahead=PBUF)
        o_taken = events("o_taken", ahead=1)
        inv_ok = events("inv_ok")
        o_out = [events(f"o_out{c}", 16, 1) for c in range(2)]

        waited = events("waited")

        block = ctx.enter_context(nc.Block())

        TRIPLES = (UNITS - 2) // NPACK

        def over_units(eng, unit):
            with eng.Fori(0, TRIPLES) as i:
                for r in range(NPACK):
                    unit(i * NPACK + r, r, i, True, True)
            for u in range(TRIPLES * NPACK, UNITS):
                unit(u, u % NPACK, u // NPACK, u + 1 < UNITS, u + 2 < UNITS)

        @block.sync
        def _(sp):
            def load(u, r):
                for dst, src in unit_loads(u, packs[r], q_scr, k_scr, v_scr):
                    sp.dma_start(dst, src).then_inc(loaded[r].sem, 16)

            def neg_rows(u, r, c, taken):
                sp.wait_ge(*taken)
                for part in range(2):
                    sp.dma_start(q_pack[r][KROWS + part:KROWS + part + 1, c, :, :].rearrange("a h n -> a (h n)"),
                                 neg_top[:, c, part, :]).then_inc(neg_in[c].sem, 16)

            def store(u, c, taken):
                sp.wait_ge(*taken)
                dst = o_scr[bass.ds(u, 1), c * CH:(c + 1) * CH, :].rearrange("a (t p) v -> p (a t) v", p=P)
                sp.dma_start(dst, o_rows[:, c, :, :].rearrange("p (t h) d -> p t (h d)", t=CT)).then_inc(o_out[c].sem, 16)

            def unit(u, r, i, more, more2):
                neg_rows(u, r, 1, ring_taken[u * J + (J0 + ring.index(("turn", 1)))])
                if more2:
                    sp.wait_ge(*pv_made[u * NS - 1])
                    load(u + 2, (r + 2) % NPACK)
                outs = [n for n, job in enumerate(ring_of(more)) if job[0] == "out"]
                store(u, 0, ring_taken[u * J + (J0 + outs[0])])
                if more:
                    neg_rows(u + 1, (r + 1) % NPACK, 0, ring_taken[u * J + (J0 + ring.index(("turn", 0)))])
                store(u, 1, ring_taken[u * J + (J0 + outs[1])])
                if not more2 and more:
                    sp.dma_start(w_out_raw[:, :, :], woT.rearrange("(c p) d -> p c d", p=P)).then_inc(w_loaded.sem, 16)
                    for c in range(2):
                        sp.wait_ge(*o_out[c][UNITS // BATCH - 1])
                    load_chunk(sp, 0, 0, 0, x1_scr, o_scr, o_in, x1_in, o_loaded, x1_loaded)

            load(1, 1)
            neg_rows(0, 0, 0, ring_taken[len(first)])
            over_units(sp, unit)
            for c in range(2):
                sp.wait_ge(*o_out[c][UNITS - 1])

        @block.gpsimd
        def _(pool):
            give_ahead(pool, every)
            for n in range(NPACK):
                pool.memset(k_pack[n][KROWS:SROWS, :, :], 1.0).then_inc(ones_ok.sem, 1)

            def unit(u, r, i, more, more2):
                for s in DIAG:
                    for half in range(2):
                        pool.wait_ge(*s_taken[u * 2 * NS + 2 * s + half])
                        pool.sem_inc(waited.sem, 1)
                        diagonal = probs[:, s % PBUF, 2 * half:2 * half + 2, 0:P]
                        pool.affine_select(out=diagonal, in_=diagonal, compare_op=ALU.is_ge, fill=0.0, base=0,
                                           pattern=[[0, 2], [1, P]], channel_multiplier=-1).then_inc(masked.sem, 1)

            with pool.Fori(0, UNITS) as u:
                unit(u, None, None, None, None)

        @block.scalar
        def _(act):
            def exps(u, s):
                c, kt = STEPS[s]
                width = CH - max(0, kt - CT * c) * P
                act.wait_ge(*pv_made[u * NS + s - PBUF])
                for half in range(2):
                    act.wait_ge(*s_made[u * 2 * NS + 2 * s + half])
                    act.activation(probs[:, s % PBUF, 2 * half:2 * half + 2, 0:width],
                                   ps[:, S_BANK + 2 * half:S_BANK + 2 * half + 2, 0:width], ACT.Exp).then_inc(s_taken.sem, 1)

            def take_out(u, c):
                last = [n for n, (cc, _) in enumerate(STEPS) if cc == c][-1]
                act.wait_ge(*pv_made[u * NS + last])
                act.activation(o_t[:, c, :], ps[:, O_BANK, :], ACT.Copy).then_inc(o_taken.sem, 1)

            def unit(u, more):
                for s in range(1, NS):
                    exps(u, s)
                    if s == CT:
                        take_out(u, 0)
                if more:
                    exps(u + 1, 0)
                take_out(u, 1)

            exps(0, 0)
            with act.Fori(0, UNITS - 1) as u:
                unit(u, True)
            unit(UNITS - 1, False)
            act.wait_ge(*w_loaded[0])
            act.activation(w_out[0][:, :, :], w_out_raw[:, :, :], ACT.Copy).then_inc(w_hi.sem, 1)

        @block.vector
        def _(dve):
            dve.memset(ps[:, O_BANK, :], 0.0).then_inc(ones_ok.sem, 1)

            def job(what, n, n_bank, u):
                dve.wait_ge(*ring_made[n])
                if what[0] == "max":
                    _, c, h, q, a, w = what
                    at = h * CT + q
                    if a == 0 and w == CH and c == 1:
                        dve.tensor_reduce(top[:, 1, at:at + 1], ps[:, n_bank, :], AX.X, ALU.max).then_inc(ring_taken.sem, 1)
                    else:
                        dve.sem_inc(waited.sem, 1)
                        dve.tensor_tensor_reduce(ps[:, n_bank, 0:w], ps[:, n_bank, 0:w], causal[:, CH - w:CH], 1.0, FMIN,
                                                 ALU.add, ALU.max, top[:, 2 * c, at:at + 1]).then_inc(ring_taken.sem, 1)
                elif what[0] == "turn":
                    c = what[1]
                    dve.wait_ge(*neg_in[c][(u + (1 - c)) - 1])
                    dve.tensor_scalar(neg_top[:, c, 0, :], ps[0:HG * CT, n_bank, 0:P], -1.0, None,
                                      ALU.mult).then_inc(neg_hi.sem, 1)
                    dve.wait_ge(*neg_hi[u * 2 + (2 - c)])
                    dve.scalar_tensor_tensor(out=neg_top[:, c, 1, :], in0=ps[0:HG * CT, n_bank, 0:P], scalar=-1.0,
                                             in1=neg_top[:, c, 0, :], op0=ALU.mult,
                                             op1=ALU.subtract).then_inc(ring_taken.sem, 1)
                else:
                    c = what[1]
                    banks = ps[:, n_bank, :].rearrange("p (n v) -> p n v", v=32)
                    dve.reciprocal(inv[:, c, :].unsqueeze(2), banks[:, :, HD:VC]).then_inc(inv_ok.sem, 1)
                    dve.wait_ge(*inv_ok[u * 2 + c])
                    dve.wait_ge(*o_out[c][u - 1])
                    dve.tensor_tensor(o_rows[:, c, :, :], banks[:, :, 0:HD],
                                      inv[:, c, :].unsqueeze(2).to_broadcast([P, HG * CT, HD]),
                                      ALU.mult).then_inc(ring_taken.sem, 1)

            def join_top(u, n):
                dve.wait_ge(*ring_taken[n])
                dve.tensor_tensor(top[:, 3, :], top[:, 1, :], top[:, 2, :], ALU.max).then_inc(top_ok.sem, 1)

            for n, what in enumerate(ring_start):
                job(what, n, RING + (n + SHIFT) % NRING, -1)
            join_top(0, J0 - 1)

            def unit(u, r, i, more, more2):
                for n, what in enumerate(ring_of(more)):
                    job(what, u * J + (J0 + n), bank(n), u)
                    if what == second[-1]:
                        join_top(u + 1, u * J + (J0 + n))

            with dve.Fori(0, UNITS - 1) as u:
                unit(u, None, None, True, True)
            unit(UNITS - 1, None, None, False, False)
            dve.wait_ge(*w_hi[0])
            dve.tensor_tensor(w_out[1][:, :, :], w_out_raw[:, :, :], w_out[0][:, :, :].bitcast(F32),
                              ALU.subtract).then_inc(w_cut.sem, 1)

        @block.tensor
        def _(pe):
            def job(what, n, n_bank, free, r, u, half0):
                pe.wait_ge(*ring_taken[free])
                if what[0] == "max":
                    _, c, h, q, a, w = what
                    mm = pe.matmul(ps[:, n_bank, 0:w], q_pack[r][0:KROWS, c, h, q * P:(q + 1) * P],
                                   k_pack[r][0:KROWS, h, a:a + w], start=True, stop=True)
                elif what[0] == "turn":
                    c = what[1]
                    if c == 0:
                        pe.wait_ge(*ring_taken[half0])
                    else:
                        pe.wait_ge(*top_ok[u])
                    mm = pe.transpose(ps[0:HG * CT, n_bank, 0:P], top[:, 3 * c, :], ident[:, :])
                else:
                    c = what[1]
                    pe.wait_ge(*o_taken[u * 2 + c])
                    for q in range(CT):
                        mm = pe.transpose(ps[:, n_bank, q * P:(q + 1) * P], o_t[:, c, q * P:(q + 1) * P], ident[:, :])
                mm.then_inc(ring_made.sem, 1)

            def scores(u, r, s, half):
                c, kt = STEPS[s]
                skip = max(0, kt - CT * c) * P
                if half == 0 and (s == 0 or STEPS[s - 1][0] != c):
                    pe.wait_ge(*neg_in[c][u])
                pe.wait_ge(*s_taken[u * 2 * NS + 2 * s + half - 2])
                for h in range(2 * half, 2 * half + 2):
                    mm = pe.matmul(ps[:, S_BANK + h, 0:CH - skip], k_pack[r][:, h, kt * P:(kt + 1) * P],
                                   q_pack[r][:, c, h, skip:CH], start=True, stop=True)
                mm.then_inc(s_made.sem, 1)

            def values(u, r, s):
                c, kt = STEPS[s]
                skip = max(0, kt - CT * c) * P
                if s in DIAG:
                    pe.wait_ge(*masked[(u * len(DIAG) + DIAG.index(s)) * 2 + 1])
                else:
                    pe.wait_ge(*s_taken[u * 2 * NS + 2 * s + 1])
                if kt == 0:
                    pe.wait_ge(*o_taken[u * 2 + c - 1])
                for h in range(HG):
                    mm = pe.matmul(ps[32 * h:32 * h + VC, O_BANK, skip:CH], v_pack[r][:, kt, h * VC:(h + 1) * VC],
                                   probs[:, s % PBUF, h, 0:CH - skip], start=(kt == 0),
                                   stop=(kt == CT * (c + 1) - 1))
                mm.then_inc(pv_made.sem, 1)

            pe.wait_ge(*loaded[0][0])
            for n, what in enumerate(ring_start):
                job(what, n, RING + (n + SHIFT) % NRING, n - NRING, 0, -1, len(first) - 1)
            pe.wait_ge(*ones_ok[0])
            for s in range(AHEAD):
                scores(0, 0, s, 0)
                scores(0, 0, s, 1)

            def unit(u, r, i, more, more2):
                if more:
                    nr, ni = (r + 1) % NPACK, i + (r + 1) // NPACK
                    pe.wait_ge(*loaded[nr][ni])
                n = 0
                for s in range(NS):
                    jobs = (by_step if more else tail)[s]
                    for place in range(3):
                        if place == 1:
                            values(u, r, s)
                        elif s + AHEAD < NS:
                            scores(u, r, s + AHEAD, place // 2)
                        elif more:
                            scores(u + 1, (r + 1) % NPACK, s + AHEAD - NS, place // 2)
                        for what in jobs[len(jobs) * place // 3:len(jobs) * (place + 1) // 3]:
                            job(what, u * J + (J0 + n), bank(n), u * J + (J0 + earlier(n)), (r + 1) % NPACK, u,
                                u * J + (J0 + len(first)))
                            n += 1

            over_units(pe, unit)


def stage_c(nc, shared, x1_scr, o_scr, out, start_c):
    w_out_raw, w_out, o_in, x1_in, w_loaded, w_hi, w_cut, o_loaded, x1_loaded = start_c
    ident, causal, ps, neg_half, eps, half_bias, w_ffn, a_all, a_fac, b_fac = shared
    with ExitStack() as ctx:
        every = []

        def sb(name, shape, dt=F32):
            return ctx.enter_context(nc.sbuf_tensor("c_" + name, shape, dt))

        def events(name, step=1, ahead=0):
            every.append(Events(ctx.enter_context(nc.semaphore("c_" + name)), step, ahead))
            return every[-1]

        h_t = sb("h_t", [P, GC, GT * P], F32R)
        x2 = sb("x2", [P, CT, D])
        x2_b = sb("x2_b", [P, CT, D])
        x_n = sb("x_n", [P, CT, D])
        x_t = [[sb(f"x_t{n}{h}", [P, NI, CH], F32R) for h in range(2)] for n in range(2)]
        y = sb("y", [P, 2, D])
        stats, moments = sb("stats", [P, CT, 6]), sb("moments", [P, CT, 2])
        var_eps, rstd = sb("var_eps", [P, CT]), sb("rstd", [P, CT])

        a_hi, a_cut = events("a_hi"), events("a_cut")
        h_made, h_hi, h_cut = events("h_made"), events("h_hi"), events("h_cut")
        st_ok, mom_ok, var_ok, rstd_ok, norm_ok = [events(s) for s in ("st_ok", "mom_ok", "var_ok", "rstd_ok", "norm_ok")]
        turned, t_hi, t_cut = events("turned"), events("t_hi"), events("t_cut", ahead=2)
        proj_made, proj_taken = events("proj_made", ahead=1), events("proj_taken")
        x2b_made = events("x2b_made")
        ffn_made, ffn_taken = events("ffn_made", ahead=1), events("ffn_taken", ahead=CT)
        y_out = [events(f"y_out{n}", 16, 1) for n in range(2)]

        waited = events("waited")

        block = ctx.enter_context(nc.Block())
        out_view = out.rearrange("(t p) d -> p t d", p=P)

        @block.sync
        def _(sp):
            def chunk(i, last):
                if not last:
                    sp.wait_ge(*turned[i * 2 * CT + CT - 1])
                    load_chunk(sp, i + 1, (i + 1) // 2, (i + 1) % 2, x1_scr, o_scr, o_in, x1_in, o_loaded, x1_loaded,
                               proj_taken[i * CT + CT - 1])
                for t in range(CT):
                    sp.wait_ge(*ffn_taken[i * CT + t])
                    sp.dma_start(out_view[:, bass.ds(i * CT + t, 1), :],
                                 y[:, t % 2:t % 2 + 1, :]).then_inc(y_out[t % 2].sem, 16)

            with sp.Fori(0, NCH - 1) as i:
                chunk(i, False)
            chunk(NCH - 1, True)
            for n in range(2):
                sp.wait_ge(*y_out[n][NCH * CT // 2 - 1])

        @block.gpsimd
        def _(pool):
            give_ahead(pool, every)
            with pool.Fori(0, NCH) as i:
                for t in range(CT):
                    pool.wait_ge(*mom_ok[i * CT + t])
                    pool.tensor_tensor(var_eps[:, t:t + 1], moments[:, t, 1:2], eps, ALU.add).then_inc(var_ok.sem, 1)
                    pool.wait_ge(*var_ok[i * CT + t])
                    pool.tensor_tensor(rstd[:, t:t + 1], var_eps[:, t:t + 1], neg_half, ALU.pow).then_inc(rstd_ok.sem, 1)
                    pool.wait_ge(*ffn_taken[i * CT + t - CT])
                    pool.tensor_tensor(x2_b[:, t, :], x2[:, t, :], half_bias[:, :], ALU.add).then_inc(x2b_made.sem, 1)

        @block.scalar
        def _(act):
            def turn_hi(i, n):
                act.wait_ge(*turned[i * 2 * CT + n])
                at = n % CT * P
                act.activation(x_t[n // CT][0][:, :, at:at + P], ps[:, 2 + n % 2, :].rearrange("p (c n) -> p c n", c=NI),
                               ACT.Copy).then_inc(t_hi.sem, 1)

            def turn_o(i, t):
                if t == 0:
                    act.wait_ge(*proj_made[i * CT - 1])
                turn_hi(i, t)

            def chunk(i, last):
                act.wait_ge(*ffn_made[i * CT - 1])
                for g in range(GC):
                    group_a_hi(act, a_fac, a_all, g, i * GC + g, a_hi.sem)
                for t in range(CT):
                    turn_hi(i, CT + t)
                for g in range(GC):
                    act.wait_ge(*h_made[i * GC + g])
                    act.activation(h_t[:, g, :], ps[:, g, 0:GT * P], ACT.Copy).then_inc(h_hi.sem, 1)
                if not last:
                    for t in range(CT):
                        turn_o(i + 1, t)

            for t in range(CT):
                turn_o(0, t)
            with act.Fori(0, NCH - 1) as i:
                chunk(i, False)
            chunk(NCH - 1, True)

        @block.vector
        def _(dve):
            def turn_lo(i, n):
                dve.wait_ge(*t_hi[i * 2 * CT + n])
                at = n % CT * P
                dve.tensor_tensor(x_t[n // CT][1][:, :, at:at + P], ps[:, 2 + n % 2, :].rearrange("p (c n) -> p c n", c=NI),
                                  x_t[n // CT][0][:, :, at:at + P].bitcast(F32), ALU.subtract).then_inc(t_cut.sem, 1)

            def take_ffn(i, t):
                dve.wait_ge(*ffn_made[i * CT + t])
                dve.wait_ge(*x2b_made[i * CT + t])
                dve.wait_ge(*y_out[t % 2][i * (CT // 2) + t // 2 - 1])
                dve.scalar_tensor_tensor(out=y[:, t % 2, :], in0=ps[:, 4 + t, :], scalar=0.5, in1=x2_b[:, t, :],
                                         op0=ALU.mult, op1=ALU.add).then_inc(ffn_taken.sem, 1)

            def proj_sum(i, t):
                dve.wait_ge(*proj_made[i * CT + t])
                dve.tensor_tensor(x2[:, t, :], ps[:, 4 + t, :], x1_in[:, t, :], ALU.add).then_inc(proj_taken.sem, 1)
                dve.wait_ge(*proj_taken[i * CT + t])
                dve.bn_stats(stats[:, t, :], x2[:, t, :]).then_inc(st_ok.sem, 1)
                dve.wait_ge(*st_ok[i * CT + t])
                dve.sem_inc(waited.sem, 1)
                dve.bn_aggr(moments[:, t, :], stats[:, t, :]).then_inc(mom_ok.sem, 1)

            def norm_out(i, t):
                dve.wait_ge(*rstd_ok[i * CT + t])
                dve.tensor_scalar(x_n[:, t, :], x2[:, t, :], moments[:, t, 0:1], rstd[:, t:t + 1],
                                  ALU.subtract, ALU.mult).then_inc(norm_ok.sem, 1)

            def chunk(i, last):
                for g in range(GC):
                    dve.wait_ge(*a_hi[i * GC + g])
                    group_a_lo(dve, a_fac, a_all, g, i * GC + g, a_cut.sem)
                dve.wait_ge(*x1_loaded[i])
                for t in range(CT):
                    proj_sum(i, t)
                    if t:
                        norm_out(i, t - 1)
                    if t > 1:
                        turn_lo(i, CT + t - 2)
                norm_out(i, CT - 1)
                turn_lo(i, 2 * CT - 2)
                turn_lo(i, 2 * CT - 1)
                for g in range(GC):
                    dve.wait_ge(*h_hi[i * GC + g])
                    dve.tensor_tensor(h_t[P // 2:P, g, :], ps[P // 2:P, g, 0:GT * P], h_t[P // 2:P, g, :].bitcast(F32),
                                      ALU.subtract).then_inc(h_cut.sem, 1)
                for t in range(0, CT, 2):
                    if not last:
                        turn_lo(i + 1, t)
                        turn_lo(i + 1, t + 1)
                    take_ffn(i, t)
                    take_ffn(i, t + 1)

            for t in range(CT):
                turn_lo(0, t)
            with dve.Fori(0, NCH - 1) as i:
                chunk(i, False)
            chunk(NCH - 1, True)

        @block.tensor
        def _(pe):
            def turn(i, n, source):
                pe.wait_ge(*t_cut[i * 2 * CT + n - 2])
                t = n % CT
                for ic in range(NI):
                    mm = pe.transpose(ps[:, 2 + n % 2, ic * P:(ic + 1) * P], source[:, t, ic * P:(ic + 1) * P], ident[:, :])
                mm.then_inc(turned.sem, 1)

            def ffn_base(i, t):
                pe.wait_ge(*t_cut[i * 2 * CT + CT + t])
                pe.wait_ge(*proj_taken[i * CT + t])
                project(pe, ps[:, 4 + t, :], lambda h, ic: x_t[1][h][:, ic, t * P:(t + 1) * P],
                        lambda h, ic: w_ffn[h][:, ic, :])

            def down(i, g):
                pe.wait_ge(*t_cut[i * 2 * CT + CT + (g + 1) * GT - 1])
                if g == 0:
                    pe.wait_ge(*ffn_made[i * CT - 1])
                pe.wait_ge(*a_cut[i * GC + g])
                low_rank_down(pe, ps[:, g, 0:GT * P], a_fac, x_t[1], g, h_made.sem)

            def up(i, t):
                pe.wait_ge(*h_cut[i * GC + t // GT])
                low_rank_up(pe, ps[:, 4 + t, :], h_t[:, t // GT, t % GT * P:(t % GT + 1) * P], b_fac,
                            i * GC + t // GT, ffn_made.sem)

            def turn_o(i, t):
                if t == 0:
                    pe.wait_ge(*o_loaded[i])
                turn(i, t, o_in)

            def turn_n(i, t):
                pe.wait_ge(*norm_ok[i * CT + t])
                turn(i, CT + t, x_n)

            def proj(i, t):
                pe.wait_ge(*t_cut[i * 2 * CT + t])
                pe.wait_ge(*ffn_taken[i * CT + t - CT])
                project(pe, ps[:, 4 + t, :], lambda h, ic: x_t[0][h][:, ic, t * P:(t + 1) * P],
                        lambda h, ic: w_out[h][:, ic, :], proj_made.sem)

            def chunk(i, last):
                for t in range(CT - 1):
                    proj(i, t)
                turn_n(i, 0)
                proj(i, 3)
                turn_n(i, 1)
                ffn_base(i, 0)
                turn_n(i, 2)
                ffn_base(i, 1)
                turn_n(i, 3)
                down(i, 0)
                ffn_base(i, 2)
                down(i, 1)
                if not last:
                    turn_o(i + 1, 0)
                    turn_o(i + 1, 1)
                ffn_base(i, 3)
                up(i, 0)
                up(i, 1)
                if not last:
                    turn_o(i + 1, 2)
                    turn_o(i + 1, 3)
                up(i, 2)
                up(i, 3)

            for t in range(CT):
                turn_o(0, t)
            pe.wait_ge(*w_cut[0])
            with pe.Fori(0, NCH - 1) as i:
                chunk(i, False)
            chunk(NCH - 1, True)


def kernel(L0_attn_x, L0_attn_Wq, L0_attn_bq, L0_attn_Wk, L0_attn_bk, L0_attn_Wv, L0_attn_bv, L0_attn_Wo,
           L0_attn_bo, L0_ffn_gate, L0_ffn_kernel, L0_ffn_bias, L0_ffn_lora_A, L0_ffn_lora_B,
           L0_ffn_lora_A_shared, L0_ffn_lora_B_shared):
    import numpy as np
    import concourse.bacc as bacc
    from concourse.bass_utils import run_bass_kernel_spmd

    def rows(v):
        return np.broadcast_to(np.asarray(v)[None, :], (P, D))

    shape = np.asarray(L0_attn_x).shape
    arrays = {
        "x": np.asarray(L0_attn_x).reshape(TOK, D),
        "wqT": np.asarray(L0_attn_Wq).T,
        "wkT": np.asarray(L0_attn_Wk).T,
        "wvT": np.asarray(L0_attn_Wv).T,
        "woT": np.asarray(L0_attn_Wo).T,
        "bq": np.asarray(L0_attn_bq).reshape(NI, P).T,
        "bk": np.asarray(L0_attn_bk).reshape(NI, P).T,
        "bv": rows(L0_attn_bv),
        "bo": rows(L0_attn_bo),
        "gate": np.repeat(np.asarray(L0_ffn_gate).T, RANK, axis=0),
        "ffn_w": np.asarray(L0_ffn_kernel),
        "ffn_b": rows(L0_ffn_bias),
        "lora_a": np.asarray(L0_ffn_lora_A).reshape(LORAS * RANK, D),
        "lora_b": np.asarray(L0_ffn_lora_B).transpose(0, 2, 1).reshape(LORAS * RANK, D),
        "lora_as": np.asarray(L0_ffn_lora_A_shared).T,
        "lora_bs": np.asarray(L0_ffn_lora_B_shared).T,
    }
    arrays = {n: np.ascontiguousarray(a) for n, a in arrays.items()}
    nc = bacc.Bacc("TRN2", target_bir_lowering=False, num_devices=1)
    args = [nc.dram_tensor(n, a.shape, mybir.dt.from_np(a.dtype), kind="ExternalInput").ap()
            for n, a in arrays.items()]
    out = nc.dram_tensor("out", (TOK, D), F32, kind="ExternalOutput").ap()
    build(nc, *args, out)
    r = run_bass_kernel_spmd(nc, [arrays], core_ids=[0])
    return r.results[0]["out"].reshape(shape)
```
